# Optimizing a Trainium2 kernel written in Bass

```python
import numpy as np
import jax
import jax.numpy as jnp

def _softmax(x, axis=-1):
    return jax.nn.softmax(x, axis=axis)

def _gelu(x):
    return jax.nn.gelu(x, approximate=True)

def _silu(x):
    return jax.nn.silu(x)

def _sigmoid(x):
    return jax.nn.sigmoid(x)

def _layernorm(x, axis=-1, eps=1e-05):
    m = jnp.mean(x, axis=axis, keepdims=True)
    v = jnp.var(x, axis=axis, keepdims=True)
    return (x - m) / jnp.sqrt(v + eps)

def _scatter_add(tgt, idx, src, axis=0):
    return tgt.at[idx].add(src)

def _segment_sum(src, seg, n):
    return jax.ops.segment_sum(src, seg, n)
kernel_name = 'mk_xattn_seq_d2_seqx_r8_ac713a'

def setup_inputs(seed: int=0):
    np.random.seed(seed)
    _w = jnp.asarray

    def _rec_inputs():
        import jax
        import jax.numpy as jnp
        _rk = jax.random.key(seed)
        x = 7.22e-05 + 1 * jax.random.normal(jax.random.fold_in(_rk, 1), (128, 64, 128), jnp.float32)
        _lenS = 64 - jax.random.randint(jax.random.fold_in(_rk, 7), (128,), 0, max(1, 64 // 4) + 1, jnp.int32)
        _lenS2 = 64 - jax.random.randint(jax.random.fold_in(_rk, 8), (128,), 0, max(1, 64 // 4) + 1, jnp.int32)
        _ctx_512P = jax.random.normal(jax.random.fold_in(_rk, 11), (128, 16, 64), jnp.float32)
        _ctx_512c = jax.random.dirichlet(jax.random.fold_in(_rk, 511), 0.3 * jnp.ones((16,), jnp.float32), (128, 64))
        _ctx_512t = jnp.einsum('bsk,bkd->bsd', _ctx_512c, _ctx_512P)
        _ctx_512t = _ctx_512t * jax.lax.rsqrt(jnp.mean(jnp.square(_ctx_512t)) + 1e-12) * 0.953939
        ctx_512 = 4.13588e-05 + 0.999923 * (_ctx_512t + 0.3 * jax.random.normal(jax.random.fold_in(_rk, 611), (128, 64, 64), jnp.float32))
        fside_BxSxS_0 = 0.000376506 + 0.999991 * jax.random.normal(jax.random.fold_in(_rk, 12), (128, 64, 64), jnp.float32)
        return (x, ctx_512, fside_BxSxS_0)
    x, ctx_512, fside_BxSxS_0 = _rec_inputs()

    def _L0_xattn_setup():
        import jax, jax.numpy as jnp
        import numpy as np
        EPS = 1e-05

        def _ln(x, g, b):
            mu = jnp.mean(x, axis=-1, keepdims=True)
            var = jnp.var(x, axis=-1, keepdims=True)
            return (x - mu) * jax.lax.rsqrt(var + EPS) * g + b

        def _cma(x1, x2, ln1_g, ln1_b, ln2_g, ln2_b, Wq, bq, Wk, bk, Wv, bv, Wo, bo):
            e = Wq.shape[1]
            scale = e ** (-0.5)
            x1n = _ln(x1, ln1_g, ln1_b)
            x2n = _ln(x2, ln2_g, ln2_b)
            q = x1n @ Wq + bq
            k = x2n @ Wk + bk
            v = x2n @ Wv + bv
            attn = jax.nn.softmax(jnp.einsum('bqe,bke->bqk', q, k) * scale, axis=-1)
            ctx = jnp.einsum('bqk,bke->bqe', attn, v)
            return ctx @ Wo + bo
        key = jax.random.key(seed)
        ks = jax.random.split(key, 24)
        B, Lt, La, Lv = (16, 64, 128, 64)
        Dt, Da, Dv, E = (128, 64, 64, 128)
        s = lambda k, *sh: jax.random.normal(k, sh, dtype=jnp.float32) * 0.02
        inp = {'text': jax.random.normal(ks[0], (B, Lt, Dt), dtype=jnp.float32), 'audio': jax.random.normal(ks[1], (B, La, Da), dtype=jnp.float32), 'video': jax.random.normal(ks[2], (B, Lv, Dv), dtype=jnp.float32), 'a_ln1_g': jnp.ones((Dt,)), 'a_ln1_b': jnp.zeros((Dt,)), 'a_ln2_g': jnp.ones((Da,)), 'a_ln2_b': jnp.zeros((Da,)), 'a_Wq': s(ks[3], Dt, E), 'a_bq': jnp.zeros((E,)), 'a_Wk': s(ks[4], Da, E), 'a_bk': jnp.zeros((E,)), 'a_Wv': s(ks[5], Da, E), 'a_bv': jnp.zeros((E,)), 'a_Wo': s(ks[6], E, Dt), 'a_bo': jnp.zeros((Dt,)), 'v_ln1_g': jnp.ones((Dt,)), 'v_ln1_b': jnp.zeros((Dt,)), 'v_ln2_g': jnp.ones((Dv,)), 'v_ln2_b': jnp.zeros((Dv,)), 'v_Wq': s(ks[7], Dt, E), 'v_bq': jnp.zeros((E,)), 'v_Wk': s(ks[8], Dv, E), 'v_bk': jnp.zeros((E,)), 'v_Wv': s(ks[9], Dv, E), 'v_bv': jnp.zeros((E,)), 'v_Wo': s(ks[10], E, Dt), 'v_bo': jnp.zeros((Dt,)), 'ln_g': jnp.ones((Dt,)), 'ln_b': jnp.zeros((Dt,)), 'fc_W': s(ks[11], Dt, Dt), 'fc_b': jnp.zeros((Dt,))}
        return inp
    _L0_xattn_all = _L0_xattn_setup()
    _L0_xattn_in = {k: v for k, v in _L0_xattn_all.items() if k in ('a_ln1_g', 'a_ln1_b', 'a_ln2_g', 'a_ln2_b', 'a_Wq', 'a_bq', 'a_Wk', 'a_bk', 'a_Wv', 'a_bv', 'a_Wo', 'a_bo', 'v_ln1_g', 'v_ln1_b', 'v_ln2_g', 'v_ln2_b', 'v_Wq', 'v_bq', 'v_Wk', 'v_bk', 'v_Wv', 'v_bv', 'v_Wo', 'v_bo', 'ln_g', 'ln_b', 'fc_W', 'fc_b')}
    del _L0_xattn_all

    def _L1_xattn_setup():
        import jax, jax.numpy as jnp
        import numpy as np
        QUERY_DIM = 128
        KEY_DIM = 64
        HIDDEN_DIM = 128
        B, LQ, LK = (8, 256, 256)
        key = jax.random.key(seed)
        ks = jax.random.split(key, 10)
        s_q = 1.0 / np.sqrt(QUERY_DIM)
        s_k = 1.0 / np.sqrt(KEY_DIM)
        s_h = 1.0 / np.sqrt(HIDDEN_DIM)
        return {'query': jax.random.normal(ks[0], (B, LQ, QUERY_DIM), jnp.float32), 'key': jax.random.normal(ks[1], (B, LK, KEY_DIM), jnp.float32), 'Wq': jax.random.uniform(ks[2], (QUERY_DIM, HIDDEN_DIM), jnp.float32, -s_q, s_q), 'bq': jax.random.uniform(ks[3], (HIDDEN_DIM,), jnp.float32, -s_q, s_q), 'Wk': jax.random.uniform(ks[4], (KEY_DIM, HIDDEN_DIM), jnp.float32, -s_k, s_k), 'bk': jax.random.uniform(ks[5], (HIDDEN_DIM,), jnp.float32, -s_k, s_k), 'Wv': jax.random.uniform(ks[6], (KEY_DIM, HIDDEN_DIM), jnp.float32, -s_k, s_k), 'bv': jax.random.uniform(ks[7], (HIDDEN_DIM,), jnp.float32, -s_k, s_k), 'Wo': jax.random.uniform(ks[8], (HIDDEN_DIM, QUERY_DIM), jnp.float32, -s_h, s_h), 'bo': jax.random.uniform(ks[9], (QUERY_DIM,), jnp.float32, -s_h, s_h)}
    _L1_xattn_all = _L1_xattn_setup()
    _L1_xattn_in = {k: v for k, v in _L1_xattn_all.items() if k in ('Wq', 'bq', 'Wk', 'bk', 'Wv', 'bv', 'Wo', 'bo')}
    del _L1_xattn_all
    return {'x': x, 'ctx_512': ctx_512, 'fside_BxSxS_0': fside_BxSxS_0, 'L0_xattn_a_ln1_g': _L0_xattn_in['a_ln1_g'], 'L0_xattn_a_ln1_b': _L0_xattn_in['a_ln1_b'], 'L0_xattn_a_ln2_g': _L0_xattn_in['a_ln2_g'], 'L0_xattn_a_ln2_b': _L0_xattn_in['a_ln2_b'], 'L0_xattn_a_Wq': _L0_xattn_in['a_Wq'], 'L0_xattn_a_bq': _L0_xattn_in['a_bq'], 'L0_xattn_a_Wk': _L0_xattn_in['a_Wk'], 'L0_xattn_a_bk': _L0_xattn_in['a_bk'], 'L0_xattn_a_Wv': _L0_xattn_in['a_Wv'], 'L0_xattn_a_bv': _L0_xattn_in['a_bv'], 'L0_xattn_a_Wo': _L0_xattn_in['a_Wo'], 'L0_xattn_a_bo': _L0_xattn_in['a_bo'], 'L0_xattn_v_ln1_g': _L0_xattn_in['v_ln1_g'], 'L0_xattn_v_ln1_b': _L0_xattn_in['v_ln1_b'], 'L0_xattn_v_ln2_g': _L0_xattn_in['v_ln2_g'], 'L0_xattn_v_ln2_b': _L0_xattn_in['v_ln2_b'], 'L0_xattn_v_Wq': _L0_xattn_in['v_Wq'], 'L0_xattn_v_bq': _L0_xattn_in['v_bq'], 'L0_xattn_v_Wk': _L0_xattn_in['v_Wk'], 'L0_xattn_v_bk': _L0_xattn_in['v_bk'], 'L0_xattn_v_Wv': _L0_xattn_in['v_Wv'], 'L0_xattn_v_bv': _L0_xattn_in['v_bv'], 'L0_xattn_v_Wo': _L0_xattn_in['v_Wo'], 'L0_xattn_v_bo': _L0_xattn_in['v_bo'], 'L0_xattn_ln_g': _L0_xattn_in['ln_g'], 'L0_xattn_ln_b': _L0_xattn_in['ln_b'], 'L0_xattn_fc_W': _L0_xattn_in['fc_W'], 'L0_xattn_fc_b': _L0_xattn_in['fc_b'], 'L1_xattn_Wq': _L1_xattn_in['Wq'], 'L1_xattn_bq': _L1_xattn_in['bq'], 'L1_xattn_Wk': _L1_xattn_in['Wk'], 'L1_xattn_bk': _L1_xattn_in['bk'], 'L1_xattn_Wv': _L1_xattn_in['Wv'], 'L1_xattn_bv': _L1_xattn_in['bv'], 'L1_xattn_Wo': _L1_xattn_in['Wo'], 'L1_xattn_bo': _L1_xattn_in['bo']}

def reference(x, ctx_512, fside_BxSxS_0, L0_xattn_a_ln1_g, L0_xattn_a_ln1_b, L0_xattn_a_ln2_g, L0_xattn_a_ln2_b, L0_xattn_a_Wq, L0_xattn_a_bq, L0_xattn_a_Wk, L0_xattn_a_bk, L0_xattn_a_Wv, L0_xattn_a_bv, L0_xattn_a_Wo, L0_xattn_a_bo, L0_xattn_v_ln1_g, L0_xattn_v_ln1_b, L0_xattn_v_ln2_g, L0_xattn_v_ln2_b, L0_xattn_v_Wq, L0_xattn_v_bq, L0_xattn_v_Wk, L0_xattn_v_bk, L0_xattn_v_Wv, L0_xattn_v_bv, L0_xattn_v_Wo, L0_xattn_v_bo, L0_xattn_ln_g, L0_xattn_ln_b, L0_xattn_fc_W, L0_xattn_fc_b, L1_xattn_Wq, L1_xattn_bq, L1_xattn_Wk, L1_xattn_bk, L1_xattn_Wv, L1_xattn_bv, L1_xattn_Wo, L1_xattn_bo):
    import jax
    import jax.numpy as jnp

    def _L0_xattn_ref(text, audio, video, a_ln1_g, a_ln1_b, a_ln2_g, a_ln2_b, a_Wq, a_bq, a_Wk, a_bk, a_Wv, a_bv, a_Wo, a_bo, v_ln1_g, v_ln1_b, v_ln2_g, v_ln2_b, v_Wq, v_bq, v_Wk, v_bk, v_Wv, v_bv, v_Wo, v_bo, ln_g, ln_b, fc_W, fc_b):
        import jax, jax.numpy as jnp
        import numpy as np
        EPS = 1e-05

        def _ln(x, g, b):
            mu = jnp.mean(x, axis=-1, keepdims=True)
            var = jnp.var(x, axis=-1, keepdims=True)
            return (x - mu) * jax.lax.rsqrt(var + EPS) * g + b

        def _cma(x1, x2, ln1_g, ln1_b, ln2_g, ln2_b, Wq, bq, Wk, bk, Wv, bv, Wo, bo):
            e = Wq.shape[1]
            scale = e ** (-0.5)
            x1n = _ln(x1, ln1_g, ln1_b)
            x2n = _ln(x2, ln2_g, ln2_b)
            q = x1n @ Wq + bq
            k = x2n @ Wk + bk
            v = x2n @ Wv + bv
            attn = jax.nn.softmax(jnp.einsum('bqe,bke->bqk', q, k) * scale, axis=-1)
            ctx = jnp.einsum('bqk,bke->bqe', attn, v)
            return ctx @ Wo + bo
        out_a = _cma(text, audio, a_ln1_g, a_ln1_b, a_ln2_g, a_ln2_b, a_Wq, a_bq, a_Wk, a_bk, a_Wv, a_bv, a_Wo, a_bo)
        out_v = _cma(text, video, v_ln1_g, v_ln1_b, v_ln2_g, v_ln2_b, v_Wq, v_bq, v_Wk, v_bk, v_Wv, v_bv, v_Wo, v_bo)
        output = out_a + out_v + text
        residual = output
        output = _ln(output, ln_g, ln_b) @ fc_W + fc_b
        return output + residual

    def _L1_xattn_ref(query, key, Wq, bq, Wk, bk, Wv, bv, Wo, bo):
        import jax, jax.numpy as jnp
        import numpy as np
        QUERY_DIM = 128
        KEY_DIM = 64
        HIDDEN_DIM = 128
        B, LQ, LK = (8, 256, 256)
        scale = HIDDEN_DIM ** (-0.5)
        Q = jnp.einsum('bqd,dh->bqh', query, Wq) + bq
        K = jnp.einsum('bkd,dh->bkh', key, Wk) + bk
        V = jnp.einsum('bkd,dh->bkh', key, Wv) + bv
        scores = jnp.einsum('bqh,bkh->bqk', Q, K) * scale
        weights = jax.nn.softmax(scores, axis=-1)
        attended = jnp.einsum('bqk,bkh->bqh', weights, V)
        out = jnp.einsum('bqh,hd->bqd', attended, Wo) + bo
        return query + out
    x = _L0_xattn_ref(x, ctx_512, fside_BxSxS_0, L0_xattn_a_ln1_g, L0_xattn_a_ln1_b, L0_xattn_a_ln2_g, L0_xattn_a_ln2_b, L0_xattn_a_Wq, L0_xattn_a_bq, L0_xattn_a_Wk, L0_xattn_a_bk, L0_xattn_a_Wv, L0_xattn_a_bv, L0_xattn_a_Wo, L0_xattn_a_bo, L0_xattn_v_ln1_g, L0_xattn_v_ln1_b, L0_xattn_v_ln2_g, L0_xattn_v_ln2_b, L0_xattn_v_Wq, L0_xattn_v_bq, L0_xattn_v_Wk, L0_xattn_v_bk, L0_xattn_v_Wv, L0_xattn_v_bv, L0_xattn_v_Wo, L0_xattn_v_bo, L0_xattn_ln_g, L0_xattn_ln_b, L0_xattn_fc_W, L0_xattn_fc_b)
    x = _L1_xattn_ref(x, ctx_512, L1_xattn_Wq, L1_xattn_bq, L1_xattn_Wk, L1_xattn_bk, L1_xattn_Wv, L1_xattn_bv, L1_xattn_Wo, L1_xattn_bo)
    return x

_drawn_inputs = setup_inputs


def setup_inputs(seed=0):
    import zlib

    import numpy as np

    out = dict(_drawn_inputs(seed))
    spreads = {'L0_xattn_a_ln1_g': (1.0, 0.6),
     'L0_xattn_a_ln1_b': (0.0, 0.8),
     'L0_xattn_a_ln2_g': (1.0, 0.6),
     'L0_xattn_a_ln2_b': (0.0, 0.8),
     'L0_xattn_a_bq': (0.0, 2.0),
     'L0_xattn_a_bk': (0.0, 2.0),
     'L0_xattn_a_bv': (0.0, 0.388),
     'L0_xattn_a_bo': (0.0, 0.1),
     'L0_xattn_v_ln1_g': (1.0, 0.6),
     'L0_xattn_v_ln1_b': (0.0, 0.8),
     'L0_xattn_v_ln2_g': (1.0, 0.6),
     'L0_xattn_v_ln2_b': (0.0, 0.8),
     'L0_xattn_v_bq': (0.0, 0.8),
     'L0_xattn_v_bk': (0.0, 2.0),
     'L0_xattn_v_bv': (0.0, 0.416),
     'L0_xattn_v_bo': (0.0, 0.1),
     'L0_xattn_ln_g': (1.0, 0.595),
     'L0_xattn_ln_b': (0.0, 0.399),
     'L0_xattn_fc_b': (0.0, 0.1)}
    factors = {'fside_BxSxS_0': 8.0,
     'L0_xattn_a_Wq': 8.0,
     'L0_xattn_a_Wk': 8.0,
     'L0_xattn_a_Wv': 2.867,
     'L0_xattn_v_Wq': 8.0,
     'L0_xattn_v_Wk': 8.0,
     'L0_xattn_v_Wv': 8.0,
     'L0_xattn_v_Wo': 3.211,
     'L1_xattn_bq': 48.847,
     'L1_xattn_bk': 64.0}
    for name, (base, spread) in spreads.items():
        noise = np.random.default_rng([zlib.crc32(name.encode()), seed]).standard_normal(out[name].shape)
        drawn = base * np.exp(spread * noise) if base else spread * noise
        out[name] = jnp.asarray(drawn.astype(out[name].dtype))
    for name, factor in factors.items():
        out[name] = (out[name] * factor).astype(out[name].dtype)
    return out
```

```python
import numpy as np
from contextlib import ExitStack

import concourse.bass as bass
from concourse import mybir

F32 = mybir.dt.float32
ACT = mybir.ActivationFunctionType
ALU = mybir.AluOpType
AX = mybir.AxisListType

BATCH, S, D, C, E = 128, 64, 128, 64, 128
P = 128
PAIRS = 4
GROUPS = BATCH // (2 * PAIRS)
DUOS = PAIRS // 2
SCALE = float(E) ** -0.5
EPS = 1e-5

LAG_NORM, LAG_SCORE, LAG_MIX, LAG_DENSE, LAG_ATT1, LAG_FINAL = range(6)
STEPS = GROUPS + LAG_FINAL
LOOP_FROM = LAG_FINAL + 1
SLOTS = 2

COLS128 = ["a_ln1_g", "a_ln1_b", "v_ln1_g", "v_ln1_b", "ln_g", "ln_b",
           "a_bq", "a_bk", "a_bv", "v_bq", "v_bk", "v_bv", "1_bq", "1_bk", "1_bv", "1_bo"]
COLS64 = ["a_ln2_g", "a_ln2_b", "v_ln2_g", "v_ln2_b"]
ROWS = ["a_bo", "v_bo", "fc_b", "1_bo"]
W128 = ["a_Wq", "a_Wo", "v_Wq", "v_Wo", "fc_W", "1_Wq", "1_WqT", "1_Wo"]
W64 = ["a_Wk", "a_Wv", "v_Wk", "v_Wv"]
WT = ["1_WkT", "1_WvT", "1_WvT"]


def live(n, lag):
    return not isinstance(n, int) or 0 <= n - lag < GROUPS


def landed(g, slot):
    return (16 // SLOTS) * g + (16 - (16 // SLOTS) * slot)


def schedule(eng, step):
    for n in range(LOOP_FROM):
        step(n, n % SLOTS)
    with eng.Fori(LOOP_FROM, GROUPS - SLOTS + 1, SLOTS) as i:
        for k in range(SLOTS):
            step(i + k, (LOOP_FROM + k) % SLOTS)
    for n in range(GROUPS, STEPS):
        step(n, n % SLOTS)


def need(eng, sem, value):
    if not isinstance(value, int) or value > 0:
        eng.wait_ge(sem, value)


def attention_kernel(nc, x, cf, ct, c1, w128, w64, wt, cols128, cols64, rows, out):
    with ExitStack() as ctx:
        def sb(name, shape):
            return ctx.enter_context(nc.sbuf_tensor(name, shape, F32))

        def sem(name):
            return ctx.enter_context(nc.semaphore(name))

        w128_sb = sb("w128_sb", [P, len(W128), 128])
        w64_sb = sb("w64_sb", [C, len(W64), 128])
        wt_sb = sb("wt_sb", [E, len(WT), C])
        cols128_sb = sb("cols128_sb", [P, len(COLS128)])
        cols64_sb = sb("cols64_sb", [C, len(COLS64)])
        rows_sb = sb("rows_sb", [1, len(ROWS), 128])
        ident = sb("ident", [P, P])
        centre128 = sb("centre128", [P, P])
        centre64 = sb("centre64", [C, C])
        part_row = sb("part_row", [1, 2, P])
        cols128_d = sb("cols128_d", [P, len(COLS128)])
        cols128_c = sb("cols128_c", [P, len(COLS128)])
        cols64_c = sb("cols64_c", [C, len(COLS64)])
        affine = {s: sb(f"affine_{s}", [P, P]) for s in ("a1", "v1", "ln")}
        affine.update({s: sb(f"affine_{s}", [C, C]) for s in ("a2", "v2")})
        wqT = {s: sb(f"wqT_{s}", [E, D]) for s in "av"}
        wkT = {s: sb(f"wkT_{s}", [E, C]) for s in "av"}
        wvT = {s: sb(f"wvT_{s}", [E, C]) for s in "av"}
        wk1T = sb("wk1T", [E, C + 1])
        bv1_wide = sb("bv1_wide", [E, P])
        ones = sb("ones", [E, P])
        out1_bias = sb("out1_bias", [D, 1])
        bq1 = sb("bq1", [E, 1])
        m0 = sb("m0", [D, 2 * C])
        w0 = sb("w0", [2 * C, D])
        w_fc = sb("w_fc", [D, D])
        m1 = sb("m1", [D, C + 1])
        t1_bias = sb("t1_bias", [C + 1, 1])
        w1 = sb("w1", [2 * C, D])
        inv_n = sb("inv_n", [P, 3 * PAIRS])
        minus_half = sb("minus_half", [P, 3 * PAIRS])

        x_sb = sb("x_sb", [P, SLOTS, PAIRS, D])
        xres_sb = sb("xres_sb", [P, SLOTS, PAIRS, D])
        cf_sb = sb("cf_sb", [P, SLOTS, PAIRS, 2 * C])
        ct_sb = sb("ct_sb", [C + 1, SLOTS, PAIRS, 2, S])
        c1_sb = sb("c1_sb", [P, SLOTS, DUOS, 2, C])
        stats0 = sb("stats0", [P, SLOTS, 3 * PAIRS, 6])
        st_sum = sb("st_sum", [P, 3 * PAIRS, 2])
        st_diff = sb("st_diff", [P, 3 * PAIRS])
        st_diff2 = sb("st_diff2", [P, 3 * PAIRS])
        st_within = sb("st_within", [P, 3 * PAIRS])
        st_between = sb("st_between", [P, 3 * PAIRS])
        st_var = sb("st_var", [P, 3 * PAIRS])
        st_sr = sb("st_sr", [P, 3 * PAIRS])
        rstd0 = sb("rstd0", [P, SLOTS, 3 * PAIRS])
        shift0 = sb("shift0", [P, SLOTS, 3 * PAIRS])
        z_sb = sb("z_sb", [P, SLOTS, PAIRS, D])
        cfn_sb = sb("cfn_sb", [P, SLOTS, PAIRS, 2 * C])
        zT_sb = sb("zT_sb", [D, PAIRS, 2, S])
        cfT_sb = sb("cfT_sb", [2 * C, PAIRS, 2, S])
        t0_sb = sb("t0_sb", [2 * C, PAIRS, 2, S])
        max0 = sb("max0", [P, 2 * PAIRS])
        diff0 = sb("diff0", [P, 2 * PAIRS, S])
        exp0 = sb("exp0", [P, 2 * PAIRS, S])
        sum0 = sb("sum0", [P, 2 * PAIRS])
        rsum0 = sb("rsum0", [P, 2 * PAIRS])
        prob0 = sb("prob0", [P, 2 * PAIRS, S])
        prob0T_sb = sb("prob0T_sb", [P, PAIRS, 2, S])
        mix0_sb = sb("mix0_sb", [2 * C, PAIRS, 2, S])
        res_sb = sb("res_sb", [P, SLOTS, PAIRS, D])
        stats1 = sb("stats1", [P, PAIRS, 6])
        s1_sum = sb("s1_sum", [P, PAIRS, 2])
        s1_diff = sb("s1_diff", [P, PAIRS])
        s1_diff2 = sb("s1_diff2", [P, PAIRS])
        s1_within = sb("s1_within", [P, PAIRS])
        s1_var = sb("s1_var", [P, PAIRS])
        s1_sr = sb("s1_sr", [P, PAIRS])
        rstd1 = sb("rstd1", [P, PAIRS])
        shift1 = sb("shift1", [P, PAIRS])
        z1_sb = sb("z1_sb", [P, PAIRS, D])
        z1T_sb = sb("z1T_sb", [D, PAIRS, P])
        x1_sb = sb("x1_sb", [P, SLOTS, PAIRS, D])
        x1T_sb = sb("x1T_sb", [D, PAIRS, 2, S])
        t1_sb = sb("t1_sb", [C + 1, PAIRS, 2, S])
        max1 = sb("max1", [P, PAIRS])
        diff1 = sb("diff1", [P, PAIRS, S])
        exp1 = sb("exp1", [P, PAIRS, S])
        sum1 = sb("sum1", [P, PAIRS])
        rsum1 = sb("rsum1", [P, PAIRS])
        prob1T_sb = sb("prob1T_sb", [P, DUOS, 2, S])
        mix1_sb = sb("mix1_sb", [P, DUOS, 2, S])
        out_sb = sb("out_sb", [P, SLOTS, PAIRS, D])

        ps_z = ctx.enter_context(nc.psum_tensor("ps_z", [P, 512], F32))
        ps_s0 = ctx.enter_context(nc.psum_tensor("ps_s0", [P, 512], F32))
        ps_s1 = ctx.enter_context(nc.psum_tensor("ps_s1", [P, 512], F32))
        ps_d = ctx.enter_context(nc.psum_tensor("ps_d", [P, 512], F32))
        ps_o0 = ctx.enter_context(nc.psum_tensor("ps_o0", [P, 512], F32))
        ps_g = ctx.enter_context(nc.psum_tensor("ps_g", [P, 2, 512], F32))
        ps_g1 = ctx.enter_context(nc.psum_tensor("ps_g1", [P, 512], F32))

        weights_in = sem("weights_in")
        x_in = [sem(f"x_in{s}") for s in range(SLOTS)]
        xres_in = [sem(f"xres_in{s}") for s in range(SLOTS)]
        cf_in = [sem(f"cf_in{s}") for s in range(SLOTS)]
        ct_in = [sem(f"ct_in{s}") for s in range(SLOTS)]
        c1_in = [sem(f"c1_in{s}") for s in range(SLOTS)]
        out_stored = [sem(f"out_stored{s}") for s in range(SLOTS)]
        constants_made = sem("constants_made")
        pool_setup = sem("pool_setup")
        dve_setup = sem("dve_setup")
        pe_setup = sem("pe_setup")
        zT_made, cfT_made, t0_made, s0_made = (sem(s) for s in ("zT_made", "cfT_made", "t0_made", "s0_made"))
        prob0T_made, mix0_made, out0_made = (sem(s) for s in ("prob0T_made", "mix0_made", "out0_made"))
        z1T_made, dense_made, x1T_made, t1_made = (sem(s) for s in ("z1T_made", "dense_made", "x1T_made", "t1_made"))
        s1_made, prob1T_made, mix1_made, out1_made = (sem(s) for s in ("s1_made", "prob1T_made", "mix1_made", "out1_made"))
        zT_copied, cfT_copied, t0_copied = (sem(s) for s in ("zT_copied", "cfT_copied", "t0_copied"))
        prob0T_copied, mix0_copied, z1T_copied = (sem(s) for s in ("prob0T_copied", "mix0_copied", "z1T_copied"))
        x1T_copied, t1_copied, prob1T_copied, mix1_copied = (
            sem(s) for s in ("x1T_copied", "t1_copied", "prob1T_copied", "mix1_copied"))
        exp0_done, exp1_done, z_done, z1_done = (sem(s) for s in ("exp0_done", "exp1_done", "z_done", "z1_done"))
        stats0_done, max0_done, diff0_done, sum0_done = (
            sem(s) for s in ("stats0_done", "max0_done", "diff0_done", "sum0_done"))
        rsum0_done, prob0_done, res_done, stats1_done = (
            sem(s) for s in ("rsum0_done", "prob0_done", "res_done", "stats1_done"))
        s1_sums_done, s1_parts_done, s1_var_done, s1_sr_done, shift1_done = (
            sem(s) for s in ("s1_sums_done", "s1_parts_done", "s1_var_done", "s1_sr_done", "shift1_done"))
        x1_done, max1_done, diff1_done, sum1_done, rsum1_done, final_done = (
            sem(s) for s in ("x1_done", "max1_done", "diff1_done", "sum1_done", "rsum1_done", "final_done"))
        st_sums_done, st_parts_done, st_var_done, st_rstd_done, st_sr_done = (
            sem(s) for s in ("st_sums_done", "st_parts_done", "st_var_done", "st_rstd_done", "st_sr_done"))
        st_between_done, shift0_done, cfn_done, rstd1_done = (
            sem(s) for s in ("st_between_done", "shift0_done", "cfn_done", "rstd1_done"))

        N_WEIGHT_LOADS = 6
        SETUP_MMS = ["wqT_a", "wkT_a", "wvT_a", "wqT_v", "wkT_v", "wvT_v", "out1_bias", "bq1",
                     "m0_a", "m0_v", "w0_a", "w0_v", "w_fc", "m1", "t1_bias", "w1"]

        def made(name):
            return SETUP_MMS.index(name) + 1

        def setup_ps(name):
            n = SETUP_MMS.index(name)
            bank = [ps_z, ps_s0, ps_s1, ps_d, ps_o0, ps_g[:, 0, :], ps_g[:, 1, :], ps_g1][n % 8]
            return bank[:, 0:P] if n < 8 else bank[:, 256:256 + P]

        def w(name):
            return w128_sb[:, W128.index(name), :]

        def wc(name):
            return w64_sb[:, W64.index(name), :]

        def col(tile, name, names=COLS128):
            return tile[:, names.index(name):names.index(name) + 1]

        def row(name):
            return rows_sb[0:1, ROWS.index(name), :]

        DVE_SCALED = 9
        DVE_AFFINE = DVE_SCALED + 5

        block = ctx.enter_context(nc.Block())

        @block.sync
        def _(sp):
            sp.dma_start(cols128_sb[:, :], cols128).then_inc(weights_in, 16)
            sp.dma_start(cols64_sb[:, :], cols64).then_inc(weights_in, 16)
            sp.dma_start(rows_sb[:, :, :], rows).then_inc(weights_in, 16)

            def step(n, k):
                g, slot = n, k
                if live(n, 0):
                    need(sp, z_done, g - SLOTS + 1)
                    sp.dma_start(x_sb[:, slot, :, :], x[g, :, :, :]).then_inc(x_in[slot], 16)
                    need(sp, cfn_done, g - SLOTS + 1)
                    sp.dma_start(cf_sb[:, slot, :, :], cf[g, :, :, :]).then_inc(cf_in[slot], 16)
                if isinstance(n, int) and n == 0:
                    sp.dma_start(w64_sb[:, :, :], w64).then_inc(weights_in, 16)
                    sp.dma_start(w128_sb[:, :, :], w128).then_inc(weights_in, 16)
                    sp.dma_start(wt_sb[:, :, :], wt).then_inc(weights_in, 16)
                g, slot = n - 1, (k - 1) % SLOTS
                if live(n, 1):
                    need(sp, res_done, g - SLOTS + 1)
                    sp.dma_start(xres_sb[:, slot, :, :], x[g, :, :, :]).then_inc(xres_in[slot], 16)
                g, slot = n - 3, (k - 3) % SLOTS
                if live(n, 3):
                    need(sp, mix1_made, g - SLOTS + 1)
                    sp.dma_start(ct_sb[0:C, slot, :, :, :], ct[g, :, :, :, :]).then_inc(ct_in[slot], 16)
                    sp.dma_start(c1_sb[:, slot, :, :, :], c1[g, :, :, :, :]).then_inc(c1_in[slot], 16)
                g, slot = n - LAG_FINAL - 1, (k - LAG_FINAL - 1) % SLOTS
                if live(n, LAG_FINAL + 1):
                    need(sp, final_done, g + 1)
                    sp.dma_start(out[g, :, :, :], out_sb[:, slot, :, :]).then_inc(out_stored[slot], 16)

            schedule(sp, step)
            g = GROUPS - 1
            need(sp, final_done, g + 1)
            sp.dma_start(out[g, :, :, :], out_sb[:, g % SLOTS, :, :]).then_inc(out_stored[g % SLOTS], 16)
            for slot in range(SLOTS):
                sp.wait_ge(out_stored[slot], 16 * (GROUPS // SLOTS))

        @block.gpsimd
        def _(pool):
            pool.memset(ident[:, :], 0.0).then_inc(pool_setup, 1)
            pool.memset(ones[:, :], 1.0)
            pool.memset(part_row[0:1, 0, :], 1.0 / C)
            pool.memset(part_row[0:1, 1, :], 1.0 / D)
            pool.memset(inv_n[:, 0:PAIRS], 1.0 / D)
            pool.memset(inv_n[:, PAIRS:3 * PAIRS], 1.0 / C)
            pool.memset(minus_half[:, :], -0.5)
            pool.wait_ge(pool_setup, 1)
            pool.affine_select(out=ident[:, :], in_=ident[:, :], compare_op=ALU.not_equal, fill=1.0,
                               base=0, pattern=[[-1, P]], channel_multiplier=1).then_inc(constants_made, 1)
            pool.wait_ge(constants_made, 1)

            def step(n, k):
                g, slot = n, k
                if live(n, 0):
                    pool.wait_ge(stats0_done, g + 1)
                    half0, half1 = stats0[:, slot, :, 0:3], stats0[:, slot, :, 3:6]
                    pool.tensor_tensor(st_sum[:, :, :], half0[:, :, 1:3], half1[:, :, 1:3], ALU.add)
                    pool.tensor_tensor(st_diff[:, :], half0[:, :, 1], half1[:, :, 1],
                                       ALU.subtract).then_inc(st_sums_done, 1)
                    pool.wait_ge(st_sums_done, g + 1)
                    pool.tensor_tensor(st_diff2[:, :], st_diff[:, :], st_diff[:, :], ALU.mult)
                    pool.tensor_tensor(st_within[:, :], st_sum[:, :, 1], inv_n[:, :],
                                       ALU.mult).then_inc(st_parts_done, 1)
                    pool.wait_ge(constants_made, 1)
                    pool.wait_ge(st_parts_done, g + 1)
                    pool.tensor_scalar(st_between[:, :], st_diff2[:, :], 0.25, EPS, ALU.mult,
                                       ALU.add).then_inc(st_between_done, 1)
                    pool.wait_ge(st_between_done, g + 1)
                    pool.tensor_tensor(st_var[:, :], st_within[:, :], st_between[:, :],
                                       ALU.add).then_inc(st_var_done, 1)
                    need(pool, z_done, g - SLOTS + 1)
                    pool.wait_ge(st_var_done, g + 1)
                    pool.tensor_tensor(rstd0[:, slot, :], st_var[:, :], minus_half[:, :],
                                       ALU.pow).then_inc(st_rstd_done, 1)
                    pool.wait_ge(st_rstd_done, g + 1)
                    pool.tensor_tensor(st_sr[:, :], st_sum[:, :, 0], rstd0[:, slot, :],
                                       ALU.mult).then_inc(st_sr_done, 1)
                    pool.wait_ge(constants_made, 1)
                    pool.wait_ge(st_sr_done, g + 1)
                    pool.tensor_scalar(shift0[:, slot, :], st_sr[:, :], -0.5, 1.0, ALU.mult,
                                       ALU.add).then_inc(shift0_done, 1)
                    pool.wait_ge(constants_made, 1)
                    pool.wait_ge(shift0_done, g + 1)
                    need(pool, mix0_made, g - SLOTS + 1)
                    for p in range(PAIRS):
                        for h in range(2):
                            j = (1 + h) * PAIRS + p
                            last = pool.tensor_scalar(
                                cfn_sb[:, slot, p, h * C:(h + 1) * C], cf_sb[:, slot, p, h * C:(h + 1) * C],
                                rstd0[:, slot, j:j + 1], shift0[:, slot, j:j + 1], ALU.mult, ALU.add)
                    last.then_inc(cfn_done, 1)
                g = n - LAG_MIX
                if live(n, LAG_MIX):
                    pool.wait_ge(s1_var_done, g + 1)
                    pool.tensor_tensor(rstd1[:, :], s1_var[:, :], minus_half[:, 0:PAIRS],
                                       ALU.pow).then_inc(rstd1_done, 1)

            schedule(pool, step)

        @block.scalar
        def _(act):
            act.wait_ge(dve_setup, DVE_AFFINE + len(SETUP_MMS))

            def step(n, k):
                g, slot = n - LAG_SCORE, (k - LAG_SCORE) % SLOTS
                if live(n, LAG_SCORE):
                    act.wait_ge(zT_made, g + 1)
                    nc.scalar.copy(zT_sb[:, :, :, :], ps_z[:, :].rearrange("p (a b s) -> p a b s", a=PAIRS, b=2)
                                   ).then_inc(zT_copied, 1)
                    act.wait_ge(cfT_made, g + 1)
                    nc.scalar.copy(cfT_sb[:, :, :, :], ps_s0[:, :].rearrange("p (a b s) -> p a b s", a=PAIRS, b=2)
                                   ).then_inc(cfT_copied, 1)
                g = n - LAG_DENSE
                if live(n, LAG_DENSE):
                    act.wait_ge(z1T_made, g + 1)
                    nc.scalar.copy(z1T_sb[:, :, :], ps_d[:, :].rearrange("p (a s) -> p a s", a=PAIRS)
                                   ).then_inc(z1T_copied, 1)
                g = n - LAG_MIX
                if live(n, LAG_MIX):
                    act.wait_ge(prob0T_made, g + 1)
                    nc.scalar.copy(prob0T_sb[:, :, :, :],
                                   ps_o0[:, :].rearrange("p (a b s) -> p a b s", a=PAIRS, b=2)
                                   ).then_inc(prob0T_copied, 1)
                g = n - LAG_ATT1
                if live(n, LAG_ATT1):
                    act.wait_ge(diff1_done, g + 1)
                    nc.scalar.activation(exp1[:, :, :], diff1[:, :, :], ACT.Exp).then_inc(exp1_done, 1)
                g = n - LAG_MIX
                if live(n, LAG_MIX):
                    act.wait_ge(mix0_made, g + 1)
                    nc.scalar.copy(mix0_sb[:, :, :, :].rearrange("p a b s -> p b a s"),
                                   ps_g[:, :, 0:256].rearrange("p b (a s) -> p b a s", a=PAIRS)
                                   ).then_inc(mix0_copied, 1)
                g = n - LAG_SCORE
                if live(n, LAG_SCORE):
                    act.wait_ge(t0_made, g + 1)
                    nc.scalar.copy(t0_sb[:, :, :, :], ps_z[:, :].rearrange("p (a b s) -> p a b s", a=PAIRS, b=2)
                                   ).then_inc(t0_copied, 1)
                g, slot = n, k
                if live(n, 0):
                    act.wait_ge(x_in[slot], landed(g, slot))
                    act.wait_ge(shift0_done, g + 1)
                    for p in range(PAIRS):
                        last = nc.scalar.activation(z_sb[:, slot, p, :], x_sb[:, slot, p, :], ACT.Identity,
                                                    bias=shift0[:, slot, p:p + 1], scale=rstd0[:, slot, p:p + 1])
                    last.then_inc(z_done, 1)
                g = n - LAG_ATT1
                if live(n, LAG_ATT1):
                    act.wait_ge(prob1T_made, g + 1)
                    nc.scalar.copy(prob1T_sb[:, :, :, :],
                                   ps_g1[:, 0:256].rearrange("p (a b s) -> p a b s", a=DUOS, b=2)
                                   ).then_inc(prob1T_copied, 1)
                g = n - LAG_DENSE
                if live(n, LAG_DENSE):
                    act.wait_ge(x1T_made, g + 1)
                    nc.scalar.copy(x1T_sb[:, :, :, :], ps_d[:, :].rearrange("p (a b s) -> p a b s", a=PAIRS, b=2)
                                   ).then_inc(x1T_copied, 1)
                g = n - LAG_ATT1
                if live(n, LAG_ATT1):
                    act.wait_ge(mix1_made, g + 1)
                    nc.scalar.copy(mix1_sb[:, :, :, :],
                                   ps_g1[:, 0:256].rearrange("p (a b s) -> p a b s", a=DUOS, b=2)
                                   ).then_inc(mix1_copied, 1)
                g = n - LAG_DENSE
                if live(n, LAG_DENSE):
                    act.wait_ge(t1_made, g + 1)
                    nc.scalar.activation(t1_sb[:, :, :, :],
                                         ps_d[0:C + 1, :].rearrange("p (a b s) -> p a b s", a=PAIRS, b=2),
                                         ACT.Identity, bias=t1_bias[:, :]).then_inc(t1_copied, 1)
                g = n - LAG_SCORE
                if live(n, LAG_SCORE):
                    act.wait_ge(diff0_done, g + 1)
                    nc.scalar.activation(exp0[:, :, :], diff0[:, :, :], ACT.Exp).then_inc(exp0_done, 1)
                g = n - LAG_MIX
                if live(n, LAG_MIX):
                    act.wait_ge(shift1_done, g + 1)
                    for p in range(PAIRS):
                        last = nc.scalar.activation(z1_sb[:, p, :], res_sb[:, k % SLOTS, p, :], ACT.Identity,
                                                    bias=shift1[:, p:p + 1], scale=rstd1[:, p:p + 1])
                    last.then_inc(z1_done, 1)

            schedule(act, step)

        @block.vector
        def _(dve):
            v = nc.vector
            dve.wait_ge(constants_made, 1)
            dve.wait_ge(weights_in, 16 * N_WEIGHT_LOADS)
            v.tensor_scalar_add(centre128[:, :], ident[:, :], -1.0 / D).then_inc(dve_setup, 1)
            v.tensor_scalar_add(centre64[:, :], ident[0:C, 0:C], -1.0 / C).then_inc(dve_setup, 1)
            v.tensor_scalar_mul(cols128_d[:, :], cols128_sb[:, :], 1.0 / D).then_inc(dve_setup, 1)
            v.tensor_scalar_mul(cols128_c[:, :], cols128_sb[:, :], 1.0 / C).then_inc(dve_setup, 1)
            v.tensor_scalar_mul(cols64_c[:, :], cols64_sb[:, :], 1.0 / C).then_inc(dve_setup, 1)
            v.memset(ct_sb[C:C + 1, :, :, :, :], 1.0).then_inc(dve_setup, 1)
            v.tensor_copy(wk1T[:, 0:C], wt_sb[:, 0, :]).then_inc(dve_setup, 1)
            v.tensor_copy(wk1T[:, C:C + 1], col(cols128_sb, "1_bk")).then_inc(dve_setup, 1)
            dve.wait_ge(dve_setup, DVE_SCALED - 1)
            v.tensor_scalar_mul(bv1_wide[:, :], ones[:, :], col(cols128_d, "1_bv")).then_inc(dve_setup, 1)
            for name, s in (("a1", "a_ln1"), ("v1", "v_ln1"), ("ln", "ln")):
                v.tensor_scalar(affine[name][:, :], centre128[:, :], col(cols128_sb, s + "_g"),
                                col(cols128_d, s + "_b"), ALU.mult, ALU.add).then_inc(dve_setup, 1)
            for name, s in (("a2", "a_ln2"), ("v2", "v_ln2")):
                v.tensor_scalar(affine[name][:, :], centre64[:, :], col(cols64_sb, s + "_g", COLS64),
                                col(cols64_c, s + "_b", COLS64), ALU.mult, ALU.add).then_inc(dve_setup, 1)
            for s in "av":
                for dst, what, scaled in ((wqT[s], "q", cols128_d), (wkT[s], "k", cols128_c), (wvT[s], "v", cols128_c)):
                    name = f"w{what}T_{s}"
                    dve.wait_ge(pe_setup, made(name))
                    width = D if what == "q" else C
                    v.tensor_scalar_add(dst[:, :], setup_ps(name)[:, 0:width],
                                        col(scaled, f"{s}_b{what}")).then_inc(dve_setup, 1)
            dve.wait_ge(pe_setup, made("out1_bias"))
            v.tensor_scalar_add(out1_bias[:, :], setup_ps("out1_bias")[:, 0:1],
                                col(cols128_sb, "1_bo")).then_inc(dve_setup, 1)
            dve.wait_ge(pe_setup, made("bq1"))
            v.scalar_tensor_tensor(bq1[:, :], setup_ps("bq1")[:, 0:1], -1.0, col(cols128_sb, "1_bq"),
                                   ALU.mult, ALU.add).then_inc(dve_setup, 1)
            for name, dst, src, scale in (
                    ("m0_a", m0[:, 0:C], setup_ps("m0_a")[:, 0:C], SCALE),
                    ("m0_v", m0[:, C:2 * C], setup_ps("m0_v")[:, 0:C], SCALE),
                    ("w0_a", w0[0:C, :], setup_ps("w0_a")[0:C, :], 1.0),
                    ("w0_v", w0[C:2 * C, :], setup_ps("w0_v")[C:2 * C, :], 1.0),
                    ("w_fc", w_fc[:, :], setup_ps("w_fc"), 1.0),
                    ("m1", m1[:, :], setup_ps("m1")[:, 0:C + 1], SCALE),
                    ("t1_bias", t1_bias[:, :], setup_ps("t1_bias")[0:C + 1, 0:1], SCALE),
                    ("w1", w1[:, :], setup_ps("w1"), 1.0)):
                dve.wait_ge(pe_setup, made(name))
                v.tensor_scalar_mul(dst, src, scale).then_inc(dve_setup, 1)

            def wide(ap, n):
                return ap.unsqueeze(2).broadcast_to([P, n, S])

            def step(n, k):
                g = n - LAG_MIX
                if live(n, LAG_MIX):
                    dve.wait_ge(exp0_done, g + 1)
                    v.tensor_reduce(sum0[:, :], exp0[:, :, :], AX.X, ALU.add).then_inc(sum0_done, 1)
                    dve.wait_ge(sum0_done, g + 1)
                    v.reciprocal(rsum0[:, :], sum0[:, :]).then_inc(rsum0_done, 1)
                    dve.wait_ge(rsum0_done, g + 1)
                    v.tensor_tensor(prob0[:, :, :], exp0[:, :, :], wide(rsum0[:, :], 2 * PAIRS),
                                    ALU.mult).then_inc(prob0_done, 1)
                g, slot = n - LAG_FINAL, (k - LAG_FINAL) % SLOTS
                if live(n, LAG_FINAL):
                    dve.wait_ge(out1_made, g + 1)
                    dve.wait_ge(rsum1_done, g + 1)
                    if not (isinstance(g, int) and g < SLOTS):
                        dve.wait_ge(out_stored[slot], landed(g - SLOTS, slot))
                    for p in range(PAIRS):
                        last = v.scalar_tensor_tensor(
                            out_sb[:, slot, p, :], ps_g[:, p % 2, (p // 2) * D:(p // 2 + 1) * D],
                            rsum1[:, p:p + 1], x1_sb[:, slot, p, :], ALU.mult, ALU.add)
                    last.then_inc(final_done, 1)
                g = n - LAG_ATT1
                if live(n, LAG_ATT1):
                    dve.wait_ge(s1_made, g + 1)
                    scores = ps_s1[:, 0:256].rearrange("p (a s) -> p a s", a=PAIRS)
                    v.tensor_reduce(max1[:, :], scores, AX.X, ALU.max).then_inc(max1_done, 1)
                    dve.wait_ge(max1_done, g + 1)
                    v.tensor_tensor(diff1[:, :, :], scores, wide(max1[:, :], PAIRS),
                                    ALU.subtract).then_inc(diff1_done, 1)
                g, slot = n, k
                if live(n, 0):
                    dve.wait_ge(x_in[slot], landed(g, slot))
                    need(dve, st_sr_done, g - SLOTS + 1)
                    for p in range(PAIRS):
                        v.bn_stats(stats0[:, slot, p, :], x_sb[:, slot, p, :])
                    dve.wait_ge(cf_in[slot], landed(g, slot))
                    for h in range(2):
                        for p in range(PAIRS):
                            last = v.bn_stats(stats0[:, slot, (1 + h) * PAIRS + p, :],
                                              cf_sb[:, slot, p, h * C:(h + 1) * C])
                    last.then_inc(stats0_done, 1)
                g = n - LAG_ATT1
                if live(n, LAG_ATT1):
                    dve.wait_ge(exp1_done, g + 1)
                    v.tensor_reduce(sum1[:, :], exp1[:, :, :], AX.X, ALU.add).then_inc(sum1_done, 1)
                    dve.wait_ge(sum1_done, g + 1)
                    v.reciprocal(rsum1[:, :], sum1[:, :]).then_inc(rsum1_done, 1)
                g, slot = n - LAG_DENSE, (k - LAG_DENSE) % SLOTS
                if live(n, LAG_DENSE):
                    dve.wait_ge(dense_made, g + 1)
                    v.tensor_tensor(x1_sb[:, slot, :, :], ps_d[:, :].rearrange("p (a s) -> p a s", a=PAIRS),
                                    res_sb[:, slot, :, :], ALU.add).then_inc(x1_done, 1)
                g, slot = n - LAG_MIX, (k - LAG_MIX) % SLOTS
                if live(n, LAG_MIX):
                    dve.wait_ge(out0_made, g + 1)
                    dve.wait_ge(xres_in[slot], landed(g, slot))
                    v.tensor_tensor(res_sb[:, slot, :, :], ps_o0[:, :].rearrange("p (a s) -> p a s", a=PAIRS),
                                    xres_sb[:, slot, :, :], ALU.add).then_inc(res_done, 1)
                    dve.wait_ge(res_done, g + 1)
                    for p in range(PAIRS):
                        last = v.bn_stats(stats1[:, p, :], res_sb[:, slot, p, :])
                    last.then_inc(stats1_done, 1)
                    dve.wait_ge(stats1_done, g + 1)
                    v.tensor_tensor(s1_sum[:, :, :], stats1[:, :, 1:3], stats1[:, :, 4:6], ALU.add)
                    v.tensor_tensor(s1_diff[:, :], stats1[:, :, 1], stats1[:, :, 4],
                                    ALU.subtract).then_inc(s1_sums_done, 1)
                    dve.wait_ge(s1_sums_done, g + 1)
                    v.tensor_tensor(s1_diff2[:, :], s1_diff[:, :], s1_diff[:, :], ALU.mult)
                    v.tensor_scalar(s1_within[:, :], s1_sum[:, :, 1], 1.0 / D, EPS, ALU.mult,
                                    ALU.add).then_inc(s1_parts_done, 1)
                    dve.wait_ge(s1_parts_done, g + 1)
                    v.scalar_tensor_tensor(s1_var[:, :], s1_diff2[:, :], 0.25, s1_within[:, :], ALU.mult,
                                           ALU.add).then_inc(s1_var_done, 1)
                g = n - LAG_SCORE
                if live(n, LAG_SCORE):
                    dve.wait_ge(s0_made, g + 1)
                    scores = ps_s0[:, :].rearrange("p (a s) -> p a s", a=2 * PAIRS)
                    v.tensor_reduce(max0[:, :], scores, AX.X, ALU.max).then_inc(max0_done, 1)
                    dve.wait_ge(max0_done, g + 1)
                    v.tensor_tensor(diff0[:, :, :], scores, wide(max0[:, :], 2 * PAIRS),
                                    ALU.subtract).then_inc(diff0_done, 1)
                g = n - LAG_MIX
                if live(n, LAG_MIX):
                    dve.wait_ge(rstd1_done, g + 1)
                    v.tensor_tensor(s1_sr[:, :], s1_sum[:, :, 0], rstd1[:, :], ALU.mult).then_inc(s1_sr_done, 1)
                    dve.wait_ge(s1_sr_done, g + 1)
                    v.tensor_scalar(shift1[:, :], s1_sr[:, :], -0.5, 1.0, ALU.mult,
                                    ALU.add).then_inc(shift1_done, 1)

            schedule(dve, step)

        @block.tensor
        def _(pe):
            mm = nc.tensor.matmul
            pe.wait_ge(weights_in, 16 * N_WEIGHT_LOADS)
            pe.wait_ge(constants_made, 1)
            pe.wait_ge(dve_setup, DVE_AFFINE)
            for s in "av":
                mm(setup_ps(f"wqT_{s}"), w(f"{s}_Wq"), affine[f"{s}1"][:, :], start=True, stop=True
                   ).then_inc(pe_setup, 1)
                mm(setup_ps(f"wkT_{s}")[:, 0:C], wc(f"{s}_Wk"), affine[f"{s}2"][:, :], start=True, stop=True
                   ).then_inc(pe_setup, 1)
                mm(setup_ps(f"wvT_{s}")[:, 0:C], wc(f"{s}_Wv"), affine[f"{s}2"][:, :], start=True, stop=True
                   ).then_inc(pe_setup, 1)
            mm(setup_ps("out1_bias")[:, 0:1], w("1_Wo"), col(cols128_sb, "1_bv"), start=True, stop=True
               ).then_inc(pe_setup, 1)
            pe.wait_ge(dve_setup, DVE_AFFINE + made("out1_bias"))
            mm(setup_ps("bq1")[:, 0:1], w("1_Wq"), out1_bias[:, :], start=True, stop=True).then_inc(pe_setup, 1)
            pe.wait_ge(dve_setup, DVE_AFFINE + made("bq1"))
            for s in "av":
                mm(setup_ps(f"m0_{s}")[:, 0:C], wqT[s][:, :], wkT[s][:, :], start=True, stop=True
                   ).then_inc(pe_setup, 1)
            for s, at in (("a", 0), ("v", C)):
                dst = setup_ps(f"w0_{s}")[at:at + C, :]
                mm(dst, wvT[s][:, :], w(f"{s}_Wo"), start=True, stop=False)
                mm(dst, part_row[0:1, 0, 0:C], row(f"{s}_bo"), start=False, stop=True).then_inc(pe_setup, 1)
            mm(setup_ps("w_fc"), affine["ln"][:, :], w("fc_W"), start=True, stop=False)
            mm(setup_ps("w_fc"), part_row[0:1, 1, :], row("fc_b"), start=False, stop=False)
            mm(setup_ps("w_fc"), part_row[0:1, 1, :], row("1_bo"), start=False, stop=False)
            mm(setup_ps("w_fc"), bv1_wide[:, :], w("1_Wo"), start=False, stop=True).then_inc(pe_setup, 1)
            mm(setup_ps("m1")[:, 0:C + 1], w("1_WqT"), wk1T[:, :], start=True, stop=True).then_inc(pe_setup, 1)
            mm(setup_ps("t1_bias")[0:C + 1, 0:1], wk1T[:, :], bq1[:, :], start=True, stop=True
               ).then_inc(pe_setup, 1)
            mm(setup_ps("w1"), wt_sb[:, 1:3, :], w("1_Wo"), start=True, stop=True).then_inc(pe_setup, 1)
            pe.wait_ge(dve_setup, DVE_AFFINE + len(SETUP_MMS))

            A0, V0 = slice(0, C), slice(C, 2 * C)

            def step(n, k):
                g, slot = n - LAG_SCORE, (k - LAG_SCORE) % SLOTS
                if live(n, LAG_SCORE):
                    pe.wait_ge(z_done, g + 1)
                    for p in range(PAIRS):
                        last = nc.tensor.transpose(ps_z[:, p * P:(p + 1) * P], z_sb[:, slot, p, :], ident[:, :])
                    last.then_inc(zT_made, 1)
                    pe.wait_ge(cfn_done, g + 1)
                    need(pe, diff0_done, g)
                    for p in range(PAIRS):
                        last = nc.tensor.transpose(ps_s0[:, p * P:(p + 1) * P], cfn_sb[:, slot, p, :], ident[:, :])
                    last.then_inc(cfT_made, 1)
                g, slot = n - LAG_ATT1, (k - LAG_ATT1) % SLOTS
                if live(n, LAG_ATT1):
                    pe.wait_ge(t1_copied, g + 1)
                    pe.wait_ge(ct_in[slot], landed(g, slot))
                    for p in range(PAIRS):
                        for b in range(2):
                            last = mm(ps_s1[b * S:(b + 1) * S, p * S:(p + 1) * S], t1_sb[:, p, b, :],
                                      ct_sb[:, slot, p, b, :], start=True, stop=True)
                    last.then_inc(s1_made, 1)
                g = n - LAG_DENSE
                if live(n, LAG_DENSE):
                    pe.wait_ge(z1_done, g + 1)
                    for p in range(PAIRS):
                        last = nc.tensor.transpose(ps_d[:, p * P:(p + 1) * P], z1_sb[:, p, :], ident[:, :])
                    last.then_inc(z1T_made, 1)
                g, slot = n - LAG_MIX, (k - LAG_MIX) % SLOTS
                if live(n, LAG_MIX):
                    pe.wait_ge(prob0_done, g + 1)
                    for p in range(PAIRS):
                        last = nc.tensor.transpose(ps_o0[:, p * P:(p + 1) * P], prob0[:, 2 * p:2 * p + 2, :],
                                                   ident[:, :])
                    last.then_inc(prob0T_made, 1)
                    pe.wait_ge(pe_setup, 1)
                    pe.wait_ge(prob0T_copied, g + 1)
                    need(pe, final_done, n - LAG_FINAL + 1)
                    for p in range(PAIRS):
                        for h, b in ((0, 0), (1, 1), (1, 0), (0, 1)):
                            last = mm(ps_g[h * C:(h + 1) * C, b, p * S:(p + 1) * S],
                                      cfn_sb[b * S:(b + 1) * S, slot, p, h * C:(h + 1) * C],
                                      prob0T_sb[b * S:(b + 1) * S, p, h, :], start=True, stop=True)
                    last.then_inc(mix0_made, 1)
                g = n - LAG_SCORE
                if live(n, LAG_SCORE):
                    pe.wait_ge(zT_copied, g + 1)
                    mm(ps_z[:, :], m0[:, :], zT_sb[:, :, :, :], start=True, stop=True).then_inc(t0_made, 1)
                g = n - LAG_DENSE
                if live(n, LAG_DENSE):
                    pe.wait_ge(z1T_copied, g + 1)
                    for p in range(PAIRS):
                        last = mm(ps_d[:, p * P:(p + 1) * P], z1T_sb[:, p, :], w_fc[:, :], start=True, stop=True)
                    last.then_inc(dense_made, 1)
                g = n - LAG_MIX
                if live(n, LAG_MIX):
                    pe.wait_ge(mix0_copied, g + 1)
                    for p in range(PAIRS):
                        last = mm(ps_o0[:, p * P:(p + 1) * P], mix0_sb[:, p, :, :], w0[:, :], start=True, stop=True)
                    last.then_inc(out0_made, 1)
                g = n - LAG_ATT1
                if live(n, LAG_ATT1):
                    pe.wait_ge(exp1_done, g + 1)
                    for q in range(DUOS):
                        last = nc.tensor.transpose(ps_g1[:, q * P:(q + 1) * P], exp1[:, 2 * q:2 * q + 2, :],
                                                   ident[:, :])
                    last.then_inc(prob1T_made, 1)
                g = n - LAG_DENSE
                if live(n, LAG_DENSE):
                    pe.wait_ge(x1_done, g + 1)
                    for p in range(PAIRS):
                        last = nc.tensor.transpose(ps_d[:, p * P:(p + 1) * P],
                                                   x1_sb[:, (k - LAG_DENSE) % SLOTS, p, :], ident[:, :])
                    last.then_inc(x1T_made, 1)
                g = n - LAG_SCORE
                if live(n, LAG_SCORE):
                    pe.wait_ge(pe_setup, 1)
                    pe.wait_ge(cfT_copied, g + 1)
                    pe.wait_ge(t0_copied, g + 1)
                    for p in range(PAIRS):
                        for b in range(2):
                            for rows_ in (A0, V0):
                                last = mm(ps_s0[rows_, (2 * p + b) * S:(2 * p + b + 1) * S],
                                          t0_sb[rows_, p, b, :], cfT_sb[rows_, p, b, :], start=True, stop=True)
                    last.then_inc(s0_made, 1)
                g, slot = n - LAG_ATT1, (k - LAG_ATT1) % SLOTS
                if live(n, LAG_ATT1):
                    pe.wait_ge(pe_setup, 1)
                    pe.wait_ge(prob1T_copied, g + 1)
                    pe.wait_ge(c1_in[slot], landed(g, slot))
                    for q in range(DUOS):
                        for b in range(2):
                            for rows_ in (A0, V0):
                                last = mm(ps_g1[rows_, (2 * q + b) * S:(2 * q + b + 1) * S],
                                          c1_sb[rows_, slot, q, b, :], prob1T_sb[rows_, q, b, :],
                                          start=True, stop=True)
                    last.then_inc(mix1_made, 1)
                g = n - LAG_DENSE
                if live(n, LAG_DENSE):
                    pe.wait_ge(x1T_copied, g + 1)
                    mm(ps_d[0:C + 1, :], m1[:, :], x1T_sb[:, :, :, :], start=True, stop=True
                       ).then_inc(t1_made, 1)
                g = n - LAG_ATT1
                if live(n, LAG_ATT1):
                    pe.wait_ge(mix1_copied, g + 1)
                    for q in range(DUOS):
                        for h, rows_ in ((0, A0), (1, V0)):
                            last = mm(ps_g[:, h, q * D:(q + 1) * D], mix1_sb[rows_, q, :, :], w1[rows_, :],
                                      start=True, stop=True)
                    last.then_inc(out1_made, 1)

            schedule(pe, step)


def kernel(**inputs):
    from concourse import bacc
    from concourse.bass_utils import run_bass_kernel_spmd

    a = {k: np.asarray(v) for k, v in inputs.items()}

    def take(name):
        return a["L1_xattn_" + name[2:]] if name.startswith("1_") else a["L0_xattn_" + name]

    def by_pairs(t):
        t = t.reshape(GROUPS, PAIRS, 2 * S, t.shape[-1])
        return np.ascontiguousarray(t.transpose(0, 2, 1, 3))

    x, c, f = a["x"], a["ctx_512"], a["fside_BxSxS_0"]
    c_groups = c.reshape(GROUPS, PAIRS, 2, S, C)
    arrays = {
        "x": by_pairs(x),
        "cf": by_pairs(np.concatenate([c, f], axis=-1)),
        "ct": np.ascontiguousarray(c_groups.transpose(0, 4, 1, 2, 3)),
        "c1": np.ascontiguousarray(c.reshape(GROUPS, DUOS, 2, 2, S, C).transpose(0, 2, 4, 1, 3, 5)
                                   .reshape(GROUPS, P, DUOS, 2, C)),
        "w128": np.ascontiguousarray(np.stack(
            [take(n[:-1]).T if n.endswith("T") else take(n) for n in W128], axis=1)),
        "w64": np.ascontiguousarray(np.stack([take(n) for n in W64], axis=1)),
        "wt": np.ascontiguousarray(np.stack([take(n[:-1]).T for n in WT], axis=1)),
        "cols128": np.ascontiguousarray(np.stack([take(n) for n in COLS128], axis=1)),
        "cols64": np.ascontiguousarray(np.stack([take(n) for n in COLS64], axis=1)),
        "rows": np.ascontiguousarray(np.stack([take(n) for n in ROWS])[None]),
    }
    nc = bacc.Bacc("TRN2", target_bir_lowering=False, num_devices=1)
    args = [nc.dram_tensor(f"in_{n}", v.shape, mybir.dt.from_np(v.dtype), kind="ExternalInput").ap()
            for n, v in arrays.items()]
    out = nc.dram_tensor("out", (GROUPS, P, PAIRS, D), F32, kind="ExternalOutput").ap()
    attention_kernel(nc, *args, out)
    r = run_bass_kernel_spmd(nc, [{f"in_{n}": v for n, v in arrays.items()}], core_ids=[0])
    got = np.asarray(r.results[0]["out"]).reshape(GROUPS, P, PAIRS, D)
    return np.ascontiguousarray(got.transpose(0, 2, 1, 3)).reshape(BATCH, S, D)
```

```python
import numpy as np
from contextlib import ExitStack

import concourse.bass as bass
from concourse import mybir

F32 = mybir.dt.float32
ACT = mybir.ActivationFunctionType
ALU = mybir.AluOpType
AX = mybir.AxisListType

BATCH, S, D, C, E = 128, 64, 128, 64, 128
P = 128
PAIRS = 4
GROUPS = BATCH // (2 * PAIRS)
DUOS = PAIRS // 2
SCALE = float(E) ** -0.5
EPS = 1e-5

LAG_STATS, LAG_NORM, LAG_SCORE, LAG_MIX, LAG_DENSE, LAG_ATT1, LAG_FINAL, LAG_STORE = range(8)
STEPS = GROUPS + LAG_FINAL
SLOTS = 2
LOOP_FROM = GROUPS - (GROUPS - LAG_STORE) // SLOTS * SLOTS

COLS128 = ["a_ln1_g", "a_ln1_b", "v_ln1_g", "v_ln1_b", "ln_g", "ln_b",
           "a_bq", "a_bk", "a_bv", "v_bq", "v_bk", "v_bv", "1_bq", "1_bk", "1_bv", "1_bo"]
COLS64 = ["a_ln2_g", "a_ln2_b", "v_ln2_g", "v_ln2_b"]
ROWS = ["a_bo", "v_bo", "fc_b", "1_bo"]
W_SCORE = ["a_Wq", "v_Wq"]
W128 = ["a_Wo", "v_Wo", "fc_W", "1_Wq", "1_WqT", "1_Wo"]
W64 = ["a_Wk", "a_Wv", "v_Wk", "v_Wv"]
WT = ["1_WkT", "1_WvT", "1_WvT"]


def live(n, lag):
    return not isinstance(n, int) or 0 <= n - lag < GROUPS


def landed(g, slot):
    return (16 // SLOTS) * g + (16 - (16 // SLOTS) * slot)


def schedule(eng, step):
    for n in range(1, LOOP_FROM):
        step(n, n % SLOTS)
    with eng.Fori(LOOP_FROM, GROUPS - SLOTS + 1, SLOTS) as i:
        for k in range(SLOTS):
            step(i + k, (LOOP_FROM + k) % SLOTS)
    for n in range(GROUPS, STEPS):
        step(n, n % SLOTS)


def need(eng, sem, value):
    if not isinstance(value, int):
        eng.wait_ge(sem, value)
    elif value > 0:
        eng.wait_ge(sem, min(value, GROUPS))


def attention_kernel(nc, x, cf, ct, c1, w_score, w64, w128, wt, cols128, cols64, rows, out):
    with ExitStack() as ctx:
        def sb(name, shape):
            return ctx.enter_context(nc.sbuf_tensor(name, shape, F32))

        def sem(name):
            return ctx.enter_context(nc.semaphore(name))

        w_score_sb = sb("w_score_sb", [P, len(W_SCORE), 128])
        w64_sb = sb("w64_sb", [C, len(W64), 128])
        w128_sb = sb("w128_sb", [P, len(W128), 128])
        wt_sb = sb("wt_sb", [E, len(WT), C])
        cols128_sb = sb("cols128_sb", [P, len(COLS128)])
        cols64_sb = sb("cols64_sb", [C, len(COLS64)])
        rows_sb = sb("rows_sb", [1, len(ROWS), 128])
        ident = sb("ident", [P, P])
        centre128 = sb("centre128", [P, P])
        centre64 = sb("centre64", [C, C])
        ones = sb("ones", [P, P])
        part64 = sb("part64", [1, C])
        cols128_d = sb("cols128_d", [P, len(COLS128)])
        cols128_c = sb("cols128_c", [P, len(COLS128)])
        cols64_c = sb("cols64_c", [C, len(COLS64)])
        affine = {s: sb(f"affine_{s}", [P, P]) for s in ("a1", "v1", "ln")}
        affine.update({s: sb(f"affine_{s}", [C, C]) for s in ("a2", "v2")})
        wqT = {s: sb(f"wqT_{s}", [E, D]) for s in "av"}
        wkT = {s: sb(f"wkT_{s}", [E, C]) for s in "av"}
        wvT = {s: sb(f"wvT_{s}", [E, C]) for s in "av"}
        wk1T = sb("wk1T", [E, C + 1])
        bv1_wide = sb("bv1_wide", [E, P])
        ln_b_wide = sb("ln_b_wide", [D, P])
        out1_bias = sb("out1_bias", [D, 1])
        bq1 = sb("bq1", [E, 1])
        m0 = sb("m0", [D, 2 * C])
        w0 = sb("w0", [2 * C, D])
        w_fc = sb("w_fc", [D, D])
        row_bias = sb("row_bias", [P, D])
        m1 = sb("m1", [D, C + 1])
        t1_bias = sb("t1_bias", [C + 1, 1])
        w1 = sb("w1", [2 * C, D])
        inv_n = sb("inv_n", [P, 3 * PAIRS])
        minus_half = sb("minus_half", [P, 3 * PAIRS])
        warm = sb("warm", [1, 1])

        x_sb = sb("x_sb", [P, SLOTS, PAIRS, D])
        xres_sb = sb("xres_sb", [P, SLOTS, PAIRS, D])
        cf_sb = sb("cf_sb", [P, SLOTS, PAIRS, 2, C])
        ct_sb = sb("ct_sb", [C + 1, SLOTS, PAIRS, 2, S])
        c1_sb = sb("c1_sb", [P, SLOTS, DUOS, 2, C])
        stats0 = sb("stats0", [P, SLOTS, 3 * PAIRS, 6])
        st_sum = sb("st_sum", [P, 3 * PAIRS, 2])
        st_diff = sb("st_diff", [P, 3 * PAIRS])
        st_diff2 = sb("st_diff2", [P, 3 * PAIRS])
        st_within = sb("st_within", [P, 3 * PAIRS])
        st_between = sb("st_between", [P, 3 * PAIRS])
        st_var = sb("st_var", [P, 3 * PAIRS])
        st_sr = sb("st_sr", [P, 3 * PAIRS])
        rstd0 = sb("rstd0", [P, SLOTS, 3 * PAIRS])
        shift0 = sb("shift0", [P, SLOTS, 3 * PAIRS])
        z_sb = sb("z_sb", [P, SLOTS, PAIRS, D])
        cf_scaled = sb("cf_scaled", [P, PAIRS, 2, C])
        cfn_sb = sb("cfn_sb", [P, SLOTS, PAIRS, 2, C])
        zT_sb = sb("zT_sb", [D, PAIRS, 2, S])
        cfT_sb = sb("cfT_sb", [2 * C, PAIRS, 2, S])
        t0_sb = sb("t0_sb", [2 * C, PAIRS, 2, S])
        max0 = sb("max0", [P, 2 * PAIRS])
        diff0 = sb("diff0", [P, 2 * PAIRS, S])
        exp0 = sb("exp0", [P, 2 * PAIRS, S])
        sum0 = sb("sum0", [P, 2 * PAIRS])
        rsum0 = sb("rsum0", [P, 2 * PAIRS])
        prob0 = sb("prob0", [P, 2 * PAIRS, S])
        prob0T_sb = sb("prob0T_sb", [P, PAIRS, 2, S])
        mix0_sb = sb("mix0_sb", [2 * C, PAIRS, 2, S])
        res_sb = sb("res_sb", [P, SLOTS, PAIRS, D])
        resb_sb = sb("resb_sb", [P, PAIRS, D])
        stats1 = sb("stats1", [P, PAIRS, 6])
        s1_m2 = sb("s1_m2", [P, PAIRS])
        s1_diff = sb("s1_diff", [P, PAIRS])
        s1_diff2 = sb("s1_diff2", [P, PAIRS])
        s1_within = sb("s1_within", [P, PAIRS])
        s1_var = sb("s1_var", [P, PAIRS])
        rstd1 = sb("rstd1", [P, PAIRS])
        resT_sb = sb("resT_sb", [D, PAIRS, P])
        x1_sb = sb("x1_sb", [P, SLOTS, PAIRS, D])
        x1T_sb = sb("x1T_sb", [D, PAIRS, 2, S])
        t1_sb = sb("t1_sb", [C + 1, PAIRS, 2, S])
        minus_max1 = sb("minus_max1", [P, PAIRS])
        exp1 = sb("exp1", [P, PAIRS, S])
        sum1 = sb("sum1", [P, PAIRS])
        rsum1 = sb("rsum1", [P, PAIRS])
        prob1T_sb = sb("prob1T_sb", [P, DUOS, 2, S])
        mix1_sb = sb("mix1_sb", [P, DUOS, 2, S])
        out_sb = sb("out_sb", [P, SLOTS, PAIRS, D])

        def bank(name, shape):
            return ctx.enter_context(nc.psum_tensor(name, shape, F32))

        ps_z = bank("ps_z", [P, 512])
        ps_s0 = bank("ps_s0", [P, 512])
        ps_s1 = bank("ps_s1", [P, 512])
        ps_d = bank("ps_d", [P, 512])
        ps_o0 = bank("ps_o0", [P, 512])
        ps_g = bank("ps_g", [P, 2, 512])
        ps_g1 = bank("ps_g1", [P, 512])

        first_weights_in = sem("first_weights_in")
        late_weights_in = sem("late_weights_in")
        x_in = [sem(f"x_in{s}") for s in range(SLOTS)]
        xres_in = [sem(f"xres_in{s}") for s in range(SLOTS)]
        cf_in = [sem(f"cf_in{s}") for s in range(SLOTS)]
        ct_in = [sem(f"ct_in{s}") for s in range(SLOTS)]
        c1_in = [sem(f"c1_in{s}") for s in range(SLOTS)]
        out_stored = [sem(f"out_stored{s}") for s in range(SLOTS)]
        zeros_made = sem("zeros_made")
        constants_made = sem("constants_made")
        scaled_made = sem("scaled_made")
        affines_made = sem("affines_made")
        folds_made = sem("folds_made")
        folds_copied = sem("folds_copied")
        zT_made, cfT_made, t0_made, s0_made = (sem(s) for s in ("zT_made", "cfT_made", "t0_made", "s0_made"))
        prob0T_made, mix0_made, out0_made, resT_made = (
            sem(s) for s in ("prob0T_made", "mix0_made", "out0_made", "resT_made"))
        dense_made, x1T_made, t1_made = (sem(s) for s in ("dense_made", "x1T_made", "t1_made"))
        s1_made, prob1T_made, mix1_made, out1_made = (
            sem(s) for s in ("s1_made", "prob1T_made", "mix1_made", "out1_made"))
        zT_copied, cfT_copied, t0_copied = (sem(s) for s in ("zT_copied", "cfT_copied", "t0_copied"))
        prob0T_copied, mix0_copied, resT_copied = (sem(s) for s in ("prob0T_copied", "mix0_copied", "resT_copied"))
        x1T_copied, t1_copied, prob1T_copied, mix1_copied = (
            sem(s) for s in ("x1T_copied", "t1_copied", "prob1T_copied", "mix1_copied"))
        z_done, exp0_done, exp1_done = (sem(s) for s in ("z_done", "exp0_done", "exp1_done"))
        stats0_done, max0_done, diff0_done, sum0_done, rsum0_done, prob0_done = (
            sem(s) for s in ("stats0_done", "max0_done", "diff0_done", "sum0_done", "rsum0_done", "prob0_done"))
        res_done, stats1_done, s1_sums_done, s1_parts_done, s1_var_done = (
            sem(s) for s in ("res_done", "stats1_done", "s1_sums_done", "s1_parts_done", "s1_var_done"))
        x1_done, max1_done, rsum1_done, final_done = (
            sem(s) for s in ("x1_done", "max1_done", "rsum1_done", "final_done"))
        st_sums_done, st_parts_done, st_between_done, st_var_done = (
            sem(s) for s in ("st_sums_done", "st_parts_done", "st_between_done", "st_var_done"))
        st_rstd_done, st_sr_done, shift0_done, cf_scaled_done = (
            sem(s) for s in ("st_rstd_done", "st_sr_done", "shift0_done", "cf_scaled_done"))
        cfn_done, rstd1_done, resb_done = (sem(s) for s in ("cfn_done", "rstd1_done", "resb_done"))

        FIRST_LOADS, LATE_LOADS = 4, 3
        FOLDS = ["wqT_a", "wkT_a", "wqT_v", "wkT_v", "m0_a", "m0_v",
                 "wvT_a", "wvT_v", "out1_bias", "w_fc", "row_bias", "m1", "w0_a", "w0_v", "w1", "bq1", "t1_bias"]
        N_SCORE_FOLDS = 6

        def upto(name):
            return FOLDS.index(name) + 1

        def fold_ps(name):
            n = FOLDS.index(name) % 6
            return [ps_s1[:, 0:P], ps_d[:, 0:P], ps_o0[:, 0:P], ps_g[:, 0, 0:P], ps_g[:, 1, 0:P], ps_g1[:, 0:P]][n]

        def w(name):
            if name in W_SCORE:
                return w_score_sb[:, W_SCORE.index(name), :]
            return w128_sb[:, W128.index(name), :]

        def wc(name):
            return w64_sb[:, W64.index(name), :]

        def col(tile, name, names=COLS128):
            return tile[:, names.index(name):names.index(name) + 1]

        def row(name):
            return rows_sb[0:1, ROWS.index(name), :]

        def by_pair(ps):
            return ps.rearrange("p (a s) -> p a s", a=PAIRS)

        def by_batch(ps, pairs=PAIRS):
            return ps.rearrange("p (a b s) -> p a b s", a=pairs, b=2)

        block = ctx.enter_context(nc.Block())

        @block.sync
        def _(sp):
            def load_x_cf(g, slot):
                need(sp, z_done, g - SLOTS + 1)
                sp.dma_start(x_sb[:, slot, :, :], x[g, :, :, :]).then_inc(x_in[slot], 16)
                need(sp, cf_scaled_done, g - SLOTS + 1)
                sp.dma_start(cf_sb[:, slot, :, :, :], cf[g, :, :, :, :]).then_inc(cf_in[slot], 16)

            load_x_cf(0, 0)
            sp.dma_start(cols128_sb[:, :], cols128).then_inc(first_weights_in, 16)
            sp.dma_start(cols64_sb[:, :], cols64).then_inc(first_weights_in, 16)
            sp.dma_start(w_score_sb[:, :, :], w_score).then_inc(first_weights_in, 16)
            sp.dma_start(w64_sb[:, :, :], w64).then_inc(first_weights_in, 16)

            def step(n, k):
                g, slot = n - LAG_STATS, (k - LAG_STATS) % SLOTS
                if live(n, LAG_STATS):
                    load_x_cf(g, slot)
                if isinstance(n, int) and n == 1:
                    sp.dma_start(rows_sb[:, :, :], rows).then_inc(late_weights_in, 16)
                    sp.dma_start(w128_sb[:, :, :], w128).then_inc(late_weights_in, 16)
                    sp.dma_start(wt_sb[:, :, :], wt).then_inc(late_weights_in, 16)
                g, slot = n - LAG_SCORE, (k - LAG_SCORE) % SLOTS
                if live(n, LAG_SCORE):
                    need(sp, res_done, g - SLOTS + 1)
                    sp.dma_start(xres_sb[:, slot, :, :], x[g, :, :, :]).then_inc(xres_in[slot], 16)
                g, slot = n - LAG_DENSE, (k - LAG_DENSE) % SLOTS
                if live(n, LAG_DENSE):
                    need(sp, mix1_made, g - SLOTS + 1)
                    sp.dma_start(ct_sb[0:C, slot, :, :, :], ct[g, :, :, :, :]).then_inc(ct_in[slot], 16)
                    sp.dma_start(c1_sb[:, slot, :, :, :], c1[g, :, :, :, :]).then_inc(c1_in[slot], 16)
                g, slot = n - LAG_STORE, (k - LAG_STORE) % SLOTS
                if live(n, LAG_STORE):
                    sp.wait_ge(final_done, g + 1)
                    sp.dma_start(out[g, :, :, :], out_sb[:, slot, :, :]).then_inc(out_stored[slot], 16)

            schedule(sp, step)
            g = GROUPS - 1
            sp.wait_ge(final_done, g + 1)
            sp.dma_start(out[g, :, :, :], out_sb[:, g % SLOTS, :, :]).then_inc(out_stored[g % SLOTS], 16)
            for slot in range(SLOTS):
                sp.wait_ge(out_stored[slot], 16 * (GROUPS // SLOTS))

        @block.gpsimd
        def _(pool):
            pool.memset(ident[:, :], 0.0).then_inc(zeros_made, 1)
            pool.memset(ones[:, :], 1.0)
            pool.memset(part64[:, :], 1.0 / C)
            pool.memset(inv_n[:, 0:PAIRS], 1.0 / D)
            pool.memset(inv_n[:, PAIRS:3 * PAIRS], 1.0 / C)
            pool.memset(minus_half[:, :], -0.5)
            pool.wait_ge(zeros_made, 1)
            pool.affine_select(out=ident[:, :], in_=ident[:, :], compare_op=ALU.not_equal, fill=1.0,
                               base=0, pattern=[[-1, P]], channel_multiplier=1).then_inc(constants_made, 1)
            pool.wait_ge(constants_made, 1)

            def step(n, k):
                g, slot = n - LAG_NORM, (k - LAG_NORM) % SLOTS
                if live(n, LAG_NORM):
                    pool.wait_ge(stats0_done, g + 1)
                    half0, half1 = stats0[:, slot, :, 0:3], stats0[:, slot, :, 3:6]
                    pool.tensor_tensor(st_sum[:, :, :], half0[:, :, 1:3], half1[:, :, 1:3], ALU.add)
                    pool.tensor_tensor(st_diff[:, :], half0[:, :, 1], half1[:, :, 1],
                                       ALU.subtract).then_inc(st_sums_done, 1)
                    pool.wait_ge(st_sums_done, g + 1)
                    pool.tensor_tensor(st_diff2[:, :], st_diff[:, :], st_diff[:, :], ALU.mult)
                    pool.tensor_tensor(st_within[:, :], st_sum[:, :, 1], inv_n[:, :],
                                       ALU.mult).then_inc(st_parts_done, 1)
                    pool.wait_ge(constants_made, 1)
                    pool.wait_ge(st_parts_done, g + 1)
                    pool.tensor_scalar(st_between[:, :], st_diff2[:, :], 0.25, EPS, ALU.mult,
                                       ALU.add).then_inc(st_between_done, 1)
                    pool.wait_ge(st_between_done, g + 1)
                    pool.tensor_tensor(st_var[:, :], st_within[:, :], st_between[:, :],
                                       ALU.add).then_inc(st_var_done, 1)
                    need(pool, z_done, g - SLOTS + 1)
                    pool.wait_ge(st_var_done, g + 1)
                    pool.tensor_tensor(rstd0[:, slot, :], st_var[:, :], minus_half[:, :],
                                       ALU.pow).then_inc(st_rstd_done, 1)
                    pool.wait_ge(st_rstd_done, g + 1)
                    pool.tensor_tensor(st_sr[:, :], st_sum[:, :, 0], rstd0[:, slot, :],
                                       ALU.mult).then_inc(st_sr_done, 1)
                    pool.wait_ge(constants_made, 1)
                    pool.wait_ge(st_sr_done, g + 1)
                    pool.tensor_scalar(shift0[:, slot, :], st_sr[:, :], -0.5, 1.0, ALU.mult,
                                       ALU.add).then_inc(shift0_done, 1)

                    def of_cf(st):
                        return (st[:, slot, PAIRS:3 * PAIRS].rearrange("p (h a) -> p a h", h=2)
                                .unsqueeze(3).broadcast_to([P, PAIRS, 2, C]))

                    pool.tensor_tensor(cf_scaled[:, :, :, :], cf_sb[:, slot, :, :, :], of_cf(rstd0),
                                       ALU.mult).then_inc(cf_scaled_done, 1)
                    pool.wait_ge(shift0_done, g + 1)
                    need(pool, mix0_made, g - SLOTS + 1)
                    pool.wait_ge(cf_scaled_done, g + 1)
                    pool.tensor_tensor(cfn_sb[:, slot, :, :, :], cf_scaled[:, :, :, :], of_cf(shift0),
                                       ALU.add).then_inc(cfn_done, 1)
                g, slot = n - LAG_MIX, (k - LAG_MIX) % SLOTS
                if live(n, LAG_MIX):
                    if isinstance(n, int) and n == LAG_MIX:
                        pool.wait_ge(folds_copied, upto("row_bias"))
                    need(pool, x1_done, g)
                    pool.wait_ge(res_done, g + 1)
                    pool.tensor_tensor(resb_sb[:, :, :], res_sb[:, slot, :, :],
                                       row_bias[:, :].unsqueeze(1).broadcast_to([P, PAIRS, D]),
                                       ALU.add).then_inc(resb_done, 1)
                    pool.wait_ge(s1_var_done, g + 1)
                    pool.tensor_tensor(rstd1[:, :], s1_var[:, :], minus_half[:, 0:PAIRS],
                                       ALU.pow).then_inc(rstd1_done, 1)

            schedule(pool, step)

        @block.scalar
        def _(act):
            act.wait_ge(constants_made, 1)
            nc.scalar.activation(warm[:, :], ones[0:1, 0:1], ACT.Exp)

            def copy_late_folds():
                for name, dst, src, scale, bias in (
                        ("wvT_a", wvT["a"][:, :], fold_ps("wvT_a")[:, 0:C], 1.0, col(cols128_c, "a_bv")),
                        ("wvT_v", wvT["v"][:, :], fold_ps("wvT_v")[:, 0:C], 1.0, col(cols128_c, "v_bv")),
                        ("out1_bias", out1_bias[:, :], fold_ps("out1_bias")[:, 0:1], 1.0, col(cols128_sb, "1_bo")),
                        ("w_fc", w_fc[:, :], fold_ps("w_fc"), 1.0, None),
                        ("row_bias", row_bias[:, :], fold_ps("row_bias"), 1.0, None),
                        ("m1", m1[:, :], fold_ps("m1")[:, 0:C + 1], SCALE, None),
                        ("w0_a", w0[0:C, :], fold_ps("w0_a")[0:C, :], 1.0, None),
                        ("w0_v", w0[C:2 * C, :], fold_ps("w0_v")[C:2 * C, :], 1.0, None),
                        ("w1", w1[:, :], fold_ps("w1"), 1.0, None),
                        ("bq1", bq1[:, :], fold_ps("bq1")[:, 0:1], -1.0, col(cols128_sb, "1_bq")),
                        ("t1_bias", t1_bias[:, :], fold_ps("t1_bias")[0:C + 1, 0:1], SCALE, None)):
                    act.wait_ge(folds_made, upto(name))
                    if bias is None:
                        nc.scalar.mul(dst, src, scale).then_inc(folds_copied, 1)
                    else:
                        nc.scalar.activation(dst, src, ACT.Identity, bias=bias, scale=scale
                                             ).then_inc(folds_copied, 1)

            def step(n, k):
                g = n - LAG_SCORE
                if live(n, LAG_SCORE):
                    act.wait_ge(zT_made, g + 1)
                    nc.scalar.copy(zT_sb[:, :, :, :], by_batch(ps_z[:, :])).then_inc(zT_copied, 1)
                    act.wait_ge(cfT_made, g + 1)
                    nc.scalar.copy(cfT_sb[:, :, :, :], by_batch(ps_s0[:, :])).then_inc(cfT_copied, 1)
                g = n - LAG_MIX
                if live(n, LAG_MIX):
                    act.wait_ge(prob0T_made, g + 1)
                    nc.scalar.copy(prob0T_sb[:, :, :, :], by_batch(ps_o0[:, :])).then_inc(prob0T_copied, 1)
                g = n - LAG_ATT1
                if live(n, LAG_ATT1):
                    act.wait_ge(max1_done, g + 1)
                    need(act, rsum1_done, g)
                    for p in range(PAIRS):
                        last = nc.scalar.activation(exp1[:, p, :], ps_s1[:, p * S:(p + 1) * S], ACT.Exp,
                                                    bias=minus_max1[:, p:p + 1], accum_out=sum1[:, p:p + 1])
                    last.then_inc(exp1_done, 1)
                g = n - LAG_SCORE
                if live(n, LAG_SCORE):
                    act.wait_ge(t0_made, g + 1)
                    nc.scalar.copy(t0_sb[:, :, :, :], by_batch(ps_z[:, :])).then_inc(t0_copied, 1)
                g = n - LAG_MIX
                if live(n, LAG_MIX):
                    act.wait_ge(mix0_made, g + 1)
                    nc.scalar.copy(mix0_sb[:, :, :, :].rearrange("p a b s -> p b a s"),
                                   ps_g[:, :, 0:PAIRS * S].rearrange("p b (a s) -> p b a s", a=PAIRS)
                                   ).then_inc(mix0_copied, 1)
                g = n - LAG_DENSE
                if live(n, LAG_DENSE):
                    act.wait_ge(x1T_made, g + 1)
                    nc.scalar.copy(x1T_sb[:, :, :, :], by_batch(ps_d[:, :])).then_inc(x1T_copied, 1)
                g = n - LAG_ATT1
                if live(n, LAG_ATT1):
                    act.wait_ge(prob1T_made, g + 1)
                    nc.scalar.copy(prob1T_sb[:, :, :, :], by_batch(ps_g1[:, 0:DUOS * P], DUOS)
                                   ).then_inc(prob1T_copied, 1)
                g, slot = n - LAG_NORM, (k - LAG_NORM) % SLOTS
                if live(n, LAG_NORM):
                    act.wait_ge(x_in[slot], landed(g, slot))
                    act.wait_ge(shift0_done, g + 1)
                    for p in range(PAIRS):
                        last = nc.scalar.activation(z_sb[:, slot, p, :], x_sb[:, slot, p, :], ACT.Identity,
                                                    bias=shift0[:, slot, p:p + 1], scale=rstd0[:, slot, p:p + 1])
                    last.then_inc(z_done, 1)
                g = n - LAG_ATT1
                if live(n, LAG_ATT1):
                    act.wait_ge(mix1_made, g + 1)
                    nc.scalar.copy(mix1_sb[:, :, :, :], by_batch(ps_g1[:, 0:DUOS * P], DUOS)
                                   ).then_inc(mix1_copied, 1)
                g = n - LAG_SCORE
                if live(n, LAG_SCORE):
                    act.wait_ge(diff0_done, g + 1)
                    nc.scalar.activation(exp0[:, :, :], diff0[:, :, :], ACT.Exp).then_inc(exp0_done, 1)
                g = n - LAG_DENSE
                if live(n, LAG_DENSE):
                    act.wait_ge(t1_made, g + 1)
                    nc.scalar.activation(t1_sb[:, :, :, :], by_batch(ps_d[0:C + 1, :]), ACT.Identity,
                                         bias=t1_bias[:, :]).then_inc(t1_copied, 1)
                g = n - LAG_MIX
                if live(n, LAG_MIX):
                    act.wait_ge(resT_made, g + 1)
                    nc.scalar.copy(resT_sb[:, :, :], by_pair(ps_s1[:, :])).then_inc(resT_copied, 1)
                if isinstance(n, int) and n == LAG_SCORE:
                    copy_late_folds()

            schedule(act, step)

        @block.vector
        def _(dve):
            v = nc.vector

            def wide(ap, n):
                return ap.unsqueeze(2).broadcast_to([P, n, S])

            def stats(g, slot):
                dve.wait_ge(x_in[slot], landed(g, slot))
                need(dve, st_sr_done, g - SLOTS + 1)
                for p in range(PAIRS):
                    v.bn_stats(stats0[:, slot, p, :], x_sb[:, slot, p, :])
                dve.wait_ge(cf_in[slot], landed(g, slot))
                for h in range(2):
                    for p in range(PAIRS):
                        last = v.bn_stats(stats0[:, slot, (1 + h) * PAIRS + p, :], cf_sb[:, slot, p, h, :])
                last.then_inc(stats0_done, 1)

            stats(0, 0)
            dve.wait_ge(constants_made, 1)
            v.tensor_scalar_add(centre128[:, :], ident[:, :], -1.0 / D)
            v.tensor_scalar_add(centre64[:, :], ident[0:C, 0:C], -1.0 / C)
            dve.wait_ge(first_weights_in, 16 * FIRST_LOADS)
            v.tensor_scalar_mul(cols128_d[:, :], cols128_sb[:, :], 1.0 / D)
            v.tensor_scalar_mul(cols128_c[:, :], cols128_sb[:, :], 1.0 / C)
            v.tensor_scalar_mul(cols64_c[:, :], cols64_sb[:, :], 1.0 / C).then_inc(scaled_made, 1)
            dve.wait_ge(scaled_made, 1)
            for name, s in (("a1", "a_ln1"), ("v1", "v_ln1")):
                v.tensor_scalar(affine[name][:, :], centre128[:, :], col(cols128_sb, s + "_g"),
                                col(cols128_d, s + "_b"), ALU.mult, ALU.add)
            for name, s in (("a2", "a_ln2"), ("v2", "v_ln2")):
                last = v.tensor_scalar(affine[name][:, :], centre64[:, :], col(cols64_sb, s + "_g", COLS64),
                                       col(cols64_c, s + "_b", COLS64), ALU.mult, ALU.add)
            last.then_inc(affines_made, 1)
            for s in "av":
                dve.wait_ge(folds_made, upto(f"wqT_{s}"))
                v.tensor_scalar_add(wqT[s][:, :], fold_ps(f"wqT_{s}"), col(cols128_d, f"{s}_bq")
                                    ).then_inc(folds_copied, 1)
                dve.wait_ge(folds_made, upto(f"wkT_{s}"))
                v.tensor_scalar_add(wkT[s][:, :], fold_ps(f"wkT_{s}")[:, 0:C], col(cols128_c, f"{s}_bk")
                                    ).then_inc(folds_copied, 1)
            for s, at in (("a", 0), ("v", C)):
                dve.wait_ge(folds_made, upto(f"m0_{s}"))
                v.tensor_scalar_mul(m0[:, at:at + C], fold_ps(f"m0_{s}")[:, 0:C], SCALE).then_inc(folds_copied, 1)
            v.tensor_scalar_mul(affine["ln"][:, :], centre128[:, :], col(cols128_sb, "ln_g"))
            v.tensor_scalar_mul(ln_b_wide[:, :], ones[:, :], col(cols128_sb, "ln_b"))
            v.tensor_scalar_mul(bv1_wide[:, :], ones[:, :], col(cols128_sb, "1_bv"))
            v.tensor_copy(wk1T[:, C:C + 1], col(cols128_sb, "1_bk"))
            v.memset(ct_sb[C:C + 1, :, :, :, :], 1.0)
            dve.wait_ge(late_weights_in, 16 * LATE_LOADS)
            v.tensor_copy(wk1T[:, 0:C], wt_sb[:, 0, :]).then_inc(affines_made, 1)

            def step(n, k):
                final_g, final_slot = n - LAG_FINAL, (k - LAG_FINAL) % SLOTS

                def final(pairs, first=False, done=False):
                    if not live(n, LAG_FINAL):
                        return
                    if first:
                        dve.wait_ge(out1_made, final_g + 1)
                        dve.wait_ge(rsum1_done, final_g + 1)
                        if not (isinstance(final_g, int) and final_g < SLOTS):
                            dve.wait_ge(out_stored[final_slot], landed(final_g - SLOTS, final_slot))
                    for p in pairs:
                        last = v.scalar_tensor_tensor(
                            out_sb[:, final_slot, p, :], ps_g[:, p % 2, (p // 2) * D:(p // 2 + 1) * D],
                            rsum1[:, p:p + 1], x1_sb[:, final_slot, p, :], ALU.mult, ALU.add)
                    if done:
                        last.then_inc(final_done, 1)

                g = n - LAG_MIX
                if live(n, LAG_MIX):
                    dve.wait_ge(exp0_done, g + 1)
                    v.tensor_reduce(sum0[:, :], exp0[:, :, :], AX.X, ALU.add).then_inc(sum0_done, 1)
                final([0], first=True)
                if live(n, LAG_MIX):
                    dve.wait_ge(sum0_done, g + 1)
                    v.reciprocal(rsum0[:, :], sum0[:, :]).then_inc(rsum0_done, 1)
                final([1])
                if live(n, LAG_MIX):
                    dve.wait_ge(rsum0_done, g + 1)
                    v.tensor_tensor(prob0[:, :, :], exp0[:, :, :], wide(rsum0[:, :], 2 * PAIRS),
                                    ALU.mult).then_inc(prob0_done, 1)
                final([2, 3], done=True)
                g = n - LAG_ATT1
                if live(n, LAG_ATT1):
                    dve.wait_ge(s1_made, g + 1)
                    v.tensor_reduce(minus_max1[:, :], by_pair(ps_s1[:, 0:PAIRS * S]), AX.X, ALU.max,
                                    negate=True).then_inc(max1_done, 1)
                if live(n, LAG_STATS):
                    stats(n, k)
                g, slot = n - LAG_DENSE, (k - LAG_DENSE) % SLOTS
                if live(n, LAG_DENSE):
                    dve.wait_ge(dense_made, g + 1)
                    dve.wait_ge(rstd1_done, g + 1)
                    dve.wait_ge(resb_done, g + 1)
                    need(dve, final_done, g - SLOTS + 1)
                    for p in range(PAIRS):
                        last = v.scalar_tensor_tensor(x1_sb[:, slot, p, :], ps_d[:, p * D:(p + 1) * D],
                                                      rstd1[:, p:p + 1], resb_sb[:, p, :], ALU.mult, ALU.add)
                    last.then_inc(x1_done, 1)
                g = n - LAG_ATT1
                if live(n, LAG_ATT1):
                    dve.wait_ge(exp1_done, g + 1)
                    v.reciprocal(rsum1[:, :], sum1[:, :]).then_inc(rsum1_done, 1)
                mix_g, slot = n - LAG_MIX, (k - LAG_MIX) % SLOTS
                score_g = n - LAG_SCORE
                if live(n, LAG_MIX):
                    dve.wait_ge(out0_made, mix_g + 1)
                    dve.wait_ge(xres_in[slot], landed(mix_g, slot))
                    v.tensor_tensor(res_sb[:, slot, :, :], by_pair(ps_o0[:, :]), xres_sb[:, slot, :, :],
                                    ALU.add).then_inc(res_done, 1)
                    dve.wait_ge(res_done, mix_g + 1)
                    for p in range(PAIRS):
                        last = v.bn_stats(stats1[:, p, :], res_sb[:, slot, p, :])
                    last.then_inc(stats1_done, 1)
                if live(n, LAG_SCORE):
                    dve.wait_ge(s0_made, score_g + 1)
                    v.tensor_reduce(max0[:, :], ps_s0[:, :].rearrange("p (a s) -> p a s", a=2 * PAIRS), AX.X,
                                    ALU.max).then_inc(max0_done, 1)
                if live(n, LAG_MIX):
                    dve.wait_ge(stats1_done, mix_g + 1)
                    v.tensor_tensor(s1_m2[:, :], stats1[:, :, 2], stats1[:, :, 5], ALU.add)
                    v.tensor_tensor(s1_diff[:, :], stats1[:, :, 1], stats1[:, :, 4],
                                    ALU.subtract).then_inc(s1_sums_done, 1)
                if live(n, LAG_SCORE):
                    dve.wait_ge(max0_done, score_g + 1)
                    v.tensor_tensor(diff0[:, :, :], ps_s0[:, :].rearrange("p (a s) -> p a s", a=2 * PAIRS),
                                    wide(max0[:, :], 2 * PAIRS), ALU.subtract).then_inc(diff0_done, 1)
                if live(n, LAG_MIX):
                    dve.wait_ge(s1_sums_done, mix_g + 1)
                    v.tensor_tensor(s1_diff2[:, :], s1_diff[:, :], s1_diff[:, :], ALU.mult)
                    v.tensor_scalar(s1_within[:, :], s1_m2[:, :], 1.0 / D, EPS, ALU.mult,
                                    ALU.add).then_inc(s1_parts_done, 1)
                    dve.wait_ge(s1_parts_done, mix_g + 1)
                    v.scalar_tensor_tensor(s1_var[:, :], s1_diff2[:, :], 0.25, s1_within[:, :], ALU.mult,
                                           ALU.add).then_inc(s1_var_done, 1)

            schedule(dve, step)

        @block.tensor
        def _(pe):
            mm = nc.tensor.matmul
            pe.wait_ge(constants_made, 1)
            pe.wait_ge(first_weights_in, 16 * FIRST_LOADS)
            pe.wait_ge(affines_made, 1)
            for s in "av":
                mm(fold_ps(f"wqT_{s}"), w(f"{s}_Wq"), affine[f"{s}1"][:, :], start=True, stop=True
                   ).then_inc(folds_made, 1)
                mm(fold_ps(f"wkT_{s}")[:, 0:C], wc(f"{s}_Wk"), affine[f"{s}2"][:, :], start=True, stop=True
                   ).then_inc(folds_made, 1)
            for s in "av":
                pe.wait_ge(folds_copied, upto(f"wkT_{s}"))
                mm(fold_ps(f"m0_{s}")[:, 0:C], wqT[s][:, :], wkT[s][:, :], start=True, stop=True
                   ).then_inc(folds_made, 1)

            def late_folds():
                pe.wait_ge(affines_made, 2)
                pe.wait_ge(late_weights_in, 16 * LATE_LOADS)
                for s in "av":
                    mm(fold_ps(f"wvT_{s}")[:, 0:C], wc(f"{s}_Wv"), affine[f"{s}2"][:, :], start=True, stop=True
                       ).then_inc(folds_made, 1)
                mm(fold_ps("out1_bias")[:, 0:1], w("1_Wo"), col(cols128_sb, "1_bv"), start=True, stop=True
                   ).then_inc(folds_made, 1)
                mm(fold_ps("w_fc"), affine["ln"][:, :], w("fc_W"), start=True, stop=True).then_inc(folds_made, 1)
                dst = fold_ps("row_bias")
                mm(dst, ln_b_wide[:, :], w("fc_W"), start=True, stop=False)
                mm(dst, bv1_wide[:, :], w("1_Wo"), start=False, stop=False)
                mm(dst, ones[0:1, :], row("fc_b"), start=False, stop=False)
                mm(dst, ones[0:1, :], row("1_bo"), start=False, stop=True).then_inc(folds_made, 1)
                mm(fold_ps("m1")[:, 0:C + 1], w("1_WqT"), wk1T[:, :], start=True, stop=True
                   ).then_inc(folds_made, 1)
                for s, at in (("a", 0), ("v", C)):
                    pe.wait_ge(folds_copied, upto(f"wvT_{s}"))
                    dst = fold_ps(f"w0_{s}")[at:at + C, :]
                    mm(dst, wvT[s][:, :], w(f"{s}_Wo"), start=True, stop=False)
                    mm(dst, part64[:, :], row(f"{s}_bo"), start=False, stop=True).then_inc(folds_made, 1)
                pe.wait_ge(folds_copied, upto("out1_bias"))
                mm(fold_ps("w1"), wt_sb[:, 1:3, :], w("1_Wo"), start=True, stop=True).then_inc(folds_made, 1)
                pe.wait_ge(folds_copied, upto("w_fc"))
                mm(fold_ps("bq1")[:, 0:1], w("1_Wq"), out1_bias[:, :], start=True, stop=True
                   ).then_inc(folds_made, 1)
                pe.wait_ge(folds_copied, upto("bq1"))
                mm(fold_ps("t1_bias")[0:C + 1, 0:1], wk1T[:, :], bq1[:, :], start=True, stop=True
                   ).then_inc(folds_made, 1)
                pe.wait_ge(folds_copied, len(FOLDS))

            LOW, HIGH = slice(0, C), slice(C, 2 * C)

            def step(n, k):
                score_g, score_slot = n - LAG_SCORE, (k - LAG_SCORE) % SLOTS
                mix_g, mix_slot = n - LAG_MIX, (k - LAG_MIX) % SLOTS
                dense_g, dense_slot = n - LAG_DENSE, (k - LAG_DENSE) % SLOTS
                att1_g, att1_slot = n - LAG_ATT1, (k - LAG_ATT1) % SLOTS
                if live(n, LAG_SCORE):
                    pe.wait_ge(z_done, score_g + 1)
                    for p in range(PAIRS):
                        last = nc.tensor.transpose(ps_z[:, p * P:(p + 1) * P], z_sb[:, score_slot, p, :],
                                                   ident[:, :])
                    last.then_inc(zT_made, 1)
                    pe.wait_ge(cfn_done, score_g + 1)
                    need(pe, diff0_done, score_g)
                    for p in range(PAIRS):
                        last = nc.tensor.transpose(ps_s0[:, p * P:(p + 1) * P], cfn_sb[:, score_slot, p, :, :],
                                                   ident[:, :])
                    last.then_inc(cfT_made, 1)
                if live(n, LAG_ATT1):
                    pe.wait_ge(t1_copied, att1_g + 1)
                    pe.wait_ge(ct_in[att1_slot], landed(att1_g, att1_slot))
                    need(pe, resT_copied, mix_g)
                    for p in range(PAIRS):
                        for b in range(2):
                            last = mm(ps_s1[b * S:(b + 1) * S, p * S:(p + 1) * S], t1_sb[:, p, b, :],
                                      ct_sb[:, att1_slot, p, b, :], start=True, stop=True)
                    last.then_inc(s1_made, 1)
                if live(n, LAG_MIX):
                    pe.wait_ge(prob0_done, mix_g + 1)
                    for p in range(PAIRS):
                        last = nc.tensor.transpose(ps_o0[:, p * P:(p + 1) * P], prob0[:, 2 * p:2 * p + 2, :],
                                                   ident[:, :])
                    last.then_inc(prob0T_made, 1)
                if live(n, LAG_SCORE):
                    pe.wait_ge(zT_copied, score_g + 1)
                    if isinstance(n, int) and n == LAG_SCORE:
                        pe.wait_ge(folds_copied, N_SCORE_FOLDS)
                    mm(ps_z[:, :], m0[:, :], zT_sb[:, :, :, :], start=True, stop=True).then_inc(t0_made, 1)
                if live(n, LAG_DENSE):
                    pe.wait_ge(resT_copied, dense_g + 1)
                    for p in range(PAIRS):
                        last = mm(ps_d[:, p * P:(p + 1) * P], resT_sb[:, p, :], w_fc[:, :], start=True, stop=True)
                    last.then_inc(dense_made, 1)
                if live(n, LAG_MIX):
                    pe.wait_ge(folds_made, 1)
                    need(pe, final_done, n - LAG_FINAL + 1)
                    pe.wait_ge(prob0T_copied, mix_g + 1)
                    for p in range(PAIRS):
                        for h, b in ((0, 0), (1, 1), (1, 0), (0, 1)):
                            last = mm(ps_g[h * C:(h + 1) * C, b, p * S:(p + 1) * S],
                                      cfn_sb[b * S:(b + 1) * S, mix_slot, p, h, :],
                                      prob0T_sb[b * S:(b + 1) * S, p, h, :], start=True, stop=True)
                    last.then_inc(mix0_made, 1)
                if live(n, LAG_DENSE):
                    pe.wait_ge(x1_done, dense_g + 1)
                    for p in range(PAIRS):
                        last = nc.tensor.transpose(ps_d[:, p * P:(p + 1) * P], x1_sb[:, dense_slot, p, :],
                                                   ident[:, :])
                    last.then_inc(x1T_made, 1)
                if live(n, LAG_ATT1):
                    pe.wait_ge(exp1_done, att1_g + 1)
                    for q in range(DUOS):
                        last = nc.tensor.transpose(ps_g1[:, q * P:(q + 1) * P], exp1[:, 2 * q:2 * q + 2, :],
                                                   ident[:, :])
                    last.then_inc(prob1T_made, 1)
                if live(n, LAG_MIX):
                    pe.wait_ge(mix0_copied, mix_g + 1)
                    for p in range(PAIRS):
                        last = mm(ps_o0[:, p * P:(p + 1) * P], mix0_sb[:, p, :, :], w0[:, :], start=True, stop=True)
                    last.then_inc(out0_made, 1)
                if live(n, LAG_SCORE):
                    pe.wait_ge(folds_made, 1)
                    pe.wait_ge(cfT_copied, score_g + 1)
                    pe.wait_ge(t0_copied, score_g + 1)
                    for p in range(PAIRS):
                        for b in range(2):
                            for half in (LOW, HIGH):
                                last = mm(ps_s0[half, (2 * p + b) * S:(2 * p + b + 1) * S],
                                          t0_sb[half, p, b, :], cfT_sb[half, p, b, :], start=True, stop=True)
                    last.then_inc(s0_made, 1)
                if live(n, LAG_ATT1):
                    pe.wait_ge(folds_made, 1)
                    pe.wait_ge(prob1T_copied, att1_g + 1)
                    pe.wait_ge(c1_in[att1_slot], landed(att1_g, att1_slot))
                    for q in range(DUOS):
                        for b in range(2):
                            for half in (LOW, HIGH):
                                last = mm(ps_g1[half, (2 * q + b) * S:(2 * q + b + 1) * S],
                                          c1_sb[half, att1_slot, q, b, :], prob1T_sb[half, q, b, :],
                                          start=True, stop=True)
                    last.then_inc(mix1_made, 1)
                if live(n, LAG_DENSE):
                    pe.wait_ge(x1T_copied, dense_g + 1)
                    mm(ps_d[0:C + 1, :], m1[:, :], x1T_sb[:, :, :, :], start=True, stop=True
                       ).then_inc(t1_made, 1)
                if live(n, LAG_MIX):
                    pe.wait_ge(res_done, mix_g + 1)
                    for p in range(PAIRS):
                        last = nc.tensor.transpose(ps_s1[:, p * P:(p + 1) * P], res_sb[:, mix_slot, p, :],
                                                   ident[:, :])
                    last.then_inc(resT_made, 1)
                if live(n, LAG_ATT1):
                    pe.wait_ge(mix1_copied, att1_g + 1)
                    for q in range(DUOS):
                        for h, half in ((0, LOW), (1, HIGH)):
                            last = mm(ps_g[:, h, q * D:(q + 1) * D], mix1_sb[half, q, :, :], w1[half, :],
                                      start=True, stop=True)
                    last.then_inc(out1_made, 1)
                if isinstance(n, int) and n == LAG_SCORE:
                    late_folds()

            schedule(pe, step)


def kernel(**inputs):
    from concourse import bacc
    from concourse.bass_utils import run_bass_kernel_spmd

    a = {k: np.asarray(v) for k, v in inputs.items()}

    def take(name):
        return a["L1_xattn_" + name[2:]] if name.startswith("1_") else a["L0_xattn_" + name]

    def by_pairs(t):
        t = t.reshape(GROUPS, PAIRS, 2 * S, t.shape[-1])
        return np.ascontiguousarray(t.transpose(0, 2, 1, 3))

    x, c, f = a["x"], a["ctx_512"], a["fside_BxSxS_0"]
    c_groups = c.reshape(GROUPS, PAIRS, 2, S, C)
    arrays = {
        "x": by_pairs(x),
        "cf": by_pairs(np.concatenate([c, f], axis=-1)).reshape(GROUPS, P, PAIRS, 2, C),
        "ct": np.ascontiguousarray(c_groups.transpose(0, 4, 1, 2, 3)),
        "c1": np.ascontiguousarray(c.reshape(GROUPS, DUOS, 2, 2, S, C).transpose(0, 2, 4, 1, 3, 5)
                                   .reshape(GROUPS, P, DUOS, 2, C)),
        "w_score": np.ascontiguousarray(np.stack([take(n) for n in W_SCORE], axis=1)),
        "w64": np.ascontiguousarray(np.stack([take(n) for n in W64], axis=1)),
        "w128": np.ascontiguousarray(np.stack(
            [take(n[:-1]).T if n.endswith("T") else take(n) for n in W128], axis=1)),
        "wt": np.ascontiguousarray(np.stack([take(n[:-1]).T for n in WT], axis=1)),
        "cols128": np.ascontiguousarray(np.stack([take(n) for n in COLS128], axis=1)),
        "cols64": np.ascontiguousarray(np.stack([take(n) for n in COLS64], axis=1)),
        "rows": np.ascontiguousarray(np.stack([take(n) for n in ROWS])[None]),
    }
    nc = bacc.Bacc("TRN2", target_bir_lowering=False, num_devices=1)
    args = [nc.dram_tensor(f"in_{n}", v.shape, mybir.dt.from_np(v.dtype), kind="ExternalInput").ap()
            for n, v in arrays.items()]
    out = nc.dram_tensor("out", (GROUPS, P, PAIRS, D), F32, kind="ExternalOutput").ap()
    attention_kernel(nc, *args, out)
    r = run_bass_kernel_spmd(nc, [{f"in_{n}": v for n, v in arrays.items()}], core_ids=[0])
    got = np.asarray(r.results[0]["out"]).reshape(GROUPS, P, PAIRS, D)
    return np.ascontiguousarray(got.transpose(0, 2, 1, 3)).reshape(BATCH, S, D)
```

```python
import numpy as np
from contextlib import ExitStack

import concourse.bass as bass
from concourse import mybir

F32 = mybir.dt.float32
ACT = mybir.ActivationFunctionType
ALU = mybir.AluOpType
AX = mybir.AxisListType

BATCH, S, D, C, E = 128, 64, 128, 64, 128
P = 128
PAIRS = 4
GROUPS = BATCH // (2 * PAIRS)
DUOS = PAIRS // 2
SCALE = float(E) ** -0.5
EPS = 1e-5

LAG_STATS, LAG_NORM, LAG_SCORE, LAG_MIX, LAG_DENSE, LAG_ATT1, LAG_FINAL, LAG_STORE = range(8)
STEPS = GROUPS + LAG_FINAL
SLOTS = 2
LOOP_FROM = GROUPS - (GROUPS - LAG_STORE) // SLOTS * SLOTS

COLS128 = ["a_ln1_g", "a_ln1_b", "v_ln1_g", "v_ln1_b", "ln_g", "ln_b",
           "a_bq", "a_bk", "a_bv", "v_bq", "v_bk", "v_bv", "1_bq", "1_bk", "1_bv", "1_bo"]
COLS64 = ["a_ln2_g", "a_ln2_b", "v_ln2_g", "v_ln2_b"]
ROWS = ["a_bo", "v_bo", "fc_b", "1_bo"]
W_SCORE = ["a_Wq", "v_Wq"]
W128 = ["a_Wo", "v_Wo", "fc_W", "1_Wq", "1_WqT", "1_Wo"]
W64 = ["a_Wk", "a_Wv", "v_Wk", "v_Wv"]
WT = ["1_WkT", "1_WvT", "1_WvT"]


def live(n, lag):
    return not isinstance(n, int) or 0 <= n - lag < GROUPS


def landed(g, slot):
    return (16 // SLOTS) * g + (16 - (16 // SLOTS) * slot)


def schedule(eng, step):
    for n in range(1, LOOP_FROM):
        step(n, n % SLOTS)
    with eng.Fori(LOOP_FROM, GROUPS - SLOTS + 1, SLOTS) as i:
        for k in range(SLOTS):
            step(i + k, (LOOP_FROM + k) % SLOTS)
    for n in range(GROUPS, STEPS):
        step(n, n % SLOTS)


def need(eng, sem, value):
    if not isinstance(value, int):
        eng.wait_ge(sem, value)
    elif value > 0:
        eng.wait_ge(sem, min(value, GROUPS))


def attention_kernel(nc, x, cf, ct, c1, w_score, w64, w128, wt, cols128, cols64, rows, out):
    with ExitStack() as ctx:
        def sb(name, shape):
            return ctx.enter_context(nc.sbuf_tensor(name, shape, F32))

        def sem(name):
            return ctx.enter_context(nc.semaphore(name))

        w_score_sb = sb("w_score_sb", [P, len(W_SCORE), 128])
        w64_sb = sb("w64_sb", [C, len(W64), 128])
        w128_sb = sb("w128_sb", [P, len(W128), 128])
        wt_sb = sb("wt_sb", [E, len(WT), C])
        cols128_sb = sb("cols128_sb", [P, len(COLS128)])
        cols64_sb = sb("cols64_sb", [C, len(COLS64)])
        rows_sb = sb("rows_sb", [1, len(ROWS), 128])
        ident = sb("ident", [P, P])
        centre128 = sb("centre128", [P, P])
        centre64 = sb("centre64", [C, C])
        ones = sb("ones", [P, P])
        part64 = sb("part64", [1, C])
        cols128_d = sb("cols128_d", [P, len(COLS128)])
        cols128_c = sb("cols128_c", [P, len(COLS128)])
        cols64_c = sb("cols64_c", [C, len(COLS64)])
        affine = {s: sb(f"affine_{s}", [P, P]) for s in ("a1", "v1", "ln")}
        affine.update({s: sb(f"affine_{s}", [C, C]) for s in ("a2", "v2")})
        wqT = {s: sb(f"wqT_{s}", [E, D]) for s in "av"}
        wkT = {s: sb(f"wkT_{s}", [E, C]) for s in "av"}
        wvT = {s: sb(f"wvT_{s}", [E, C]) for s in "av"}
        wk1T = sb("wk1T", [E, C + 1])
        bv1_wide = sb("bv1_wide", [E, P])
        ln_b_wide = sb("ln_b_wide", [D, P])
        out1_bias = sb("out1_bias", [D, 1])
        bq1 = sb("bq1", [E, 1])
        m0 = sb("m0", [D, 2 * C])
        w0 = sb("w0", [2 * C, D])
        w_fc = sb("w_fc", [D, D])
        row_bias = sb("row_bias", [P, D])
        m1 = sb("m1", [D, C + 1])
        t1_bias = sb("t1_bias", [C + 1, 1])
        w1 = sb("w1", [2 * C, D])
        inv_n = sb("inv_n", [P, 3 * PAIRS])
        minus_half = sb("minus_half", [P, 3 * PAIRS])
        warm = sb("warm", [1, 1])

        x_sb = sb("x_sb", [P, SLOTS, PAIRS, D])
        xres_sb = sb("xres_sb", [P, SLOTS, PAIRS, D])
        cf_sb = sb("cf_sb", [P, SLOTS, PAIRS, 2, C])
        ct_sb = sb("ct_sb", [C + 1, SLOTS, PAIRS, 2, S])
        c1_sb = sb("c1_sb", [P, SLOTS, DUOS, 2, C])
        stats0 = sb("stats0", [P, SLOTS, 3 * PAIRS, 6])
        st_sum = sb("st_sum", [P, 3 * PAIRS, 2])
        st_diff = sb("st_diff", [P, 3 * PAIRS])
        st_diff2 = sb("st_diff2", [P, 3 * PAIRS])
        st_within = sb("st_within", [P, 3 * PAIRS])
        st_between = sb("st_between", [P, 3 * PAIRS])
        st_var = sb("st_var", [P, 3 * PAIRS])
        st_sr = sb("st_sr", [P, 3 * PAIRS])
        rstd0 = sb("rstd0", [P, SLOTS, 3 * PAIRS])
        shift0 = sb("shift0", [P, SLOTS, 3 * PAIRS])
        z_sb = sb("z_sb", [P, SLOTS, PAIRS, D])
        cf_scaled = sb("cf_scaled", [P, PAIRS, 2, C])
        cfn_sb = sb("cfn_sb", [P, SLOTS, PAIRS, 2, C])
        zT_sb = sb("zT_sb", [D, PAIRS, 2, S])
        cfT_sb = sb("cfT_sb", [2 * C, PAIRS, 2, S])
        t0_sb = sb("t0_sb", [2 * C, PAIRS, 2, S])
        max0 = sb("max0", [P, 2 * PAIRS])
        diff0 = sb("diff0", [P, 2 * PAIRS, S])
        exp0 = sb("exp0", [P, 2 * PAIRS, S])
        sum0 = sb("sum0", [P, 2 * PAIRS])
        rsum0 = sb("rsum0", [P, 2 * PAIRS])
        prob0 = sb("prob0", [P, 2 * PAIRS, S])
        prob0T_sb = sb("prob0T_sb", [P, PAIRS, 2, S])
        mix0_sb = sb("mix0_sb", [2 * C, PAIRS, 2, S])
        res_sb = sb("res_sb", [P, SLOTS, PAIRS, D])
        resb_sb = sb("resb_sb", [P, PAIRS, D])
        stats1 = sb("stats1", [P, PAIRS, 6])
        s1_m2 = sb("s1_m2", [P, PAIRS])
        s1_diff = sb("s1_diff", [P, PAIRS])
        s1_diff2 = sb("s1_diff2", [P, PAIRS])
        s1_within = sb("s1_within", [P, PAIRS])
        s1_var = sb("s1_var", [P, PAIRS])
        rstd1 = sb("rstd1", [P, PAIRS])
        resT_sb = sb("resT_sb", [D, PAIRS, P])
        x1_sb = sb("x1_sb", [P, SLOTS, PAIRS, D])
        x1T_sb = sb("x1T_sb", [D, PAIRS, 2, S])
        t1_sb = sb("t1_sb", [C + 1, PAIRS, 2, S])
        minus_max1 = sb("minus_max1", [P, PAIRS])
        exp1 = sb("exp1", [P, PAIRS, S])
        sum1 = sb("sum1", [P, PAIRS])
        rsum1 = sb("rsum1", [P, PAIRS])
        prob1T_sb = sb("prob1T_sb", [P, DUOS, 2, S])
        mix1_sb = sb("mix1_sb", [P, DUOS, 2, S])
        out_sb = sb("out_sb", [P, SLOTS, PAIRS, D])

        def bank(name, shape):
            return ctx.enter_context(nc.psum_tensor(name, shape, F32))

        ps_z = bank("ps_z", [P, 512])
        ps_s0 = bank("ps_s0", [P, 512])
        ps_s1 = bank("ps_s1", [P, 512])
        ps_d = bank("ps_d", [P, 512])
        ps_o0 = bank("ps_o0", [P, 512])
        ps_g = bank("ps_g", [P, 2, 512])
        ps_g1 = bank("ps_g1", [P, 512])

        first_weights_in = sem("first_weights_in")
        late_weights_in = sem("late_weights_in")
        x_in = [sem(f"x_in{s}") for s in range(SLOTS)]
        xres_in = [sem(f"xres_in{s}") for s in range(SLOTS)]
        cf_in = [sem(f"cf_in{s}") for s in range(SLOTS)]
        ct_in = [sem(f"ct_in{s}") for s in range(SLOTS)]
        c1_in = [sem(f"c1_in{s}") for s in range(SLOTS)]
        out_stored = [sem(f"out_stored{s}") for s in range(SLOTS)]
        ct_ones_made = sem("ct_ones_made")
        zeros_made = sem("zeros_made")
        constants_made = sem("constants_made")
        scaled_made = sem("scaled_made")
        affines_made = sem("affines_made")
        folds_made = sem("folds_made")
        folds_copied = sem("folds_copied")
        late_folds_copied = sem("late_folds_copied")
        zT_made, cfT_made, t0_made, s0_made = (sem(s) for s in ("zT_made", "cfT_made", "t0_made", "s0_made"))
        prob0T_made, mix0_made, out0_made, resT_made = (
            sem(s) for s in ("prob0T_made", "mix0_made", "out0_made", "resT_made"))
        dense_made, x1T_made, t1_made = (sem(s) for s in ("dense_made", "x1T_made", "t1_made"))
        s1_made, prob1T_made, mix1_made, out1_made = (
            sem(s) for s in ("s1_made", "prob1T_made", "mix1_made", "out1_made"))
        zT_copied, cfT_copied, t0_copied = (sem(s) for s in ("zT_copied", "cfT_copied", "t0_copied"))
        prob0T_copied, mix0_copied, resT_copied = (sem(s) for s in ("prob0T_copied", "mix0_copied", "resT_copied"))
        x1T_copied, t1_copied, prob1T_copied, mix1_copied = (
            sem(s) for s in ("x1T_copied", "t1_copied", "prob1T_copied", "mix1_copied"))
        z_done, exp0_done, exp1_done = (sem(s) for s in ("z_done", "exp0_done", "exp1_done"))
        stats0_done, max0_done, diff0_done, sum0_done, rsum0_done, prob0_done = (
            sem(s) for s in ("stats0_done", "max0_done", "diff0_done", "sum0_done", "rsum0_done", "prob0_done"))
        res_done, stats1_done, s1_sums_done, s1_parts_done, s1_var_done = (
            sem(s) for s in ("res_done", "stats1_done", "s1_sums_done", "s1_parts_done", "s1_var_done"))
        x1_done, max1_done, rsum1_done, final_done = (
            sem(s) for s in ("x1_done", "max1_done", "rsum1_done", "final_done"))
        st_sums_done, st_parts_done, st_between_done, st_var_done = (
            sem(s) for s in ("st_sums_done", "st_parts_done", "st_between_done", "st_var_done"))
        st_rstd_done, st_sr_done, shift0_done, cf_scaled_done = (
            sem(s) for s in ("st_rstd_done", "st_sr_done", "shift0_done", "cf_scaled_done"))
        cfn_done, rstd1_done, resb_done = (sem(s) for s in ("cfn_done", "rstd1_done", "resb_done"))

        FIRST_LOADS, LATE_LOADS = 4, 3
        FOLDS = ["wqT_a", "wkT_a", "wqT_v", "wkT_v", "m0_a", "m0_v",
                 "wvT_a", "wvT_v", "out1_bias", "w_fc", "row_bias", "m1", "w0_a", "w0_v", "w1", "bq1", "t1_bias"]
        N_SCORE_FOLDS = 6
        N_LATE_FOLDS = len(FOLDS) - N_SCORE_FOLDS

        def upto(name):
            return FOLDS.index(name) + 1

        def upto_late(name):
            return upto(name) - N_SCORE_FOLDS

        def fold_ps(name):
            n = FOLDS.index(name) % 6
            return [ps_s1[:, 0:P], ps_d[:, 0:P], ps_o0[:, 0:P], ps_g[:, 0, 0:P], ps_g[:, 1, 0:P], ps_g1[:, 0:P]][n]

        def w(name):
            if name in W_SCORE:
                return w_score_sb[:, W_SCORE.index(name), :]
            return w128_sb[:, W128.index(name), :]

        def wc(name):
            return w64_sb[:, W64.index(name), :]

        def col(tile, name, names=COLS128):
            return tile[:, names.index(name):names.index(name) + 1]

        def row(name):
            return rows_sb[0:1, ROWS.index(name), :]

        def by_pair(ps):
            return ps.rearrange("p (a s) -> p a s", a=PAIRS)

        def by_batch(ps, pairs=PAIRS):
            return ps.rearrange("p (a b s) -> p a b s", a=pairs, b=2)

        block = ctx.enter_context(nc.Block())

        @block.sync
        def _(sp):
            def load_x_cf(g, slot):
                need(sp, cf_scaled_done, g - SLOTS + 1)
                sp.dma_start(cf_sb[:, slot, :, :, :], cf[g, :, :, :, :]).then_inc(cf_in[slot], 16)
                need(sp, z_done, g - SLOTS + 1)
                sp.dma_start(x_sb[:, slot, :, :], x[g, :, :, :]).then_inc(x_in[slot], 16)

            load_x_cf(0, 0)
            sp.dma_start(cols128_sb[:, :], cols128).then_inc(first_weights_in, 16)
            sp.dma_start(cols64_sb[:, :], cols64).then_inc(first_weights_in, 16)
            sp.dma_start(w_score_sb[:, :, :], w_score).then_inc(first_weights_in, 16)
            sp.dma_start(w64_sb[:, :, :], w64).then_inc(first_weights_in, 16)
            sp.dma_start(w128_sb[:, :, :], w128).then_inc(late_weights_in, 16)
            sp.dma_start(wt_sb[:, :, :], wt).then_inc(late_weights_in, 16)
            sp.dma_start(rows_sb[:, :, :], rows).then_inc(late_weights_in, 16)

            def step(n, k):
                g, slot = n - LAG_STATS, (k - LAG_STATS) % SLOTS
                if live(n, LAG_STATS):
                    load_x_cf(g, slot)
                g, slot = n - LAG_SCORE, (k - LAG_SCORE) % SLOTS
                if live(n, LAG_SCORE):
                    need(sp, res_done, g - SLOTS + 1)
                    sp.dma_start(xres_sb[:, slot, :, :], x[g, :, :, :]).then_inc(xres_in[slot], 16)
                g, slot = n - LAG_DENSE, (k - LAG_DENSE) % SLOTS
                if live(n, LAG_DENSE):
                    need(sp, mix1_made, g - SLOTS + 1)
                    sp.dma_start(ct_sb[0:C, slot, :, :, :], ct[g, :, :, :, :]).then_inc(ct_in[slot], 16)
                    sp.dma_start(c1_sb[:, slot, :, :, :], c1[g, :, :, :, :]).then_inc(c1_in[slot], 16)
                g, slot = n - LAG_STORE, (k - LAG_STORE) % SLOTS
                if live(n, LAG_STORE):
                    sp.wait_ge(final_done, g + 1)
                    sp.dma_start(out[g, :, :, :], out_sb[:, slot, :, :]).then_inc(out_stored[slot], 16)

            schedule(sp, step)
            g = GROUPS - 1
            sp.wait_ge(final_done, g + 1)
            sp.dma_start(out[g, :, :, :], out_sb[:, g % SLOTS, :, :]).then_inc(out_stored[g % SLOTS], 16)
            for slot in range(SLOTS):
                sp.wait_ge(out_stored[slot], 16 * (GROUPS // SLOTS))

        @block.gpsimd
        def _(pool):
            pool.memset(ident[:, :], 0.0).then_inc(zeros_made, 1)
            pool.memset(ones[:, :], 1.0)
            pool.memset(part64[:, :], 1.0 / C)
            pool.memset(inv_n[:, 0:PAIRS], 1.0 / D)
            pool.memset(inv_n[:, PAIRS:3 * PAIRS], 1.0 / C)
            pool.memset(minus_half[:, :], -0.5)
            pool.wait_ge(zeros_made, 1)
            pool.affine_select(out=ident[:, :], in_=ident[:, :], compare_op=ALU.not_equal, fill=1.0,
                               base=0, pattern=[[-1, P]], channel_multiplier=1).then_inc(constants_made, 1)
            pool.wait_ge(constants_made, 1)

            def step(n, k):
                g, slot = n - LAG_NORM, (k - LAG_NORM) % SLOTS
                if live(n, LAG_NORM):
                    pool.wait_ge(stats0_done, g + 1)
                    half0, half1 = stats0[:, slot, :, 0:3], stats0[:, slot, :, 3:6]
                    pool.tensor_tensor(st_sum[:, :, :], half0[:, :, 1:3], half1[:, :, 1:3], ALU.add)
                    pool.tensor_tensor(st_diff[:, :], half0[:, :, 1], half1[:, :, 1],
                                       ALU.subtract).then_inc(st_sums_done, 1)
                    pool.wait_ge(st_sums_done, g + 1)
                    pool.tensor_tensor(st_diff2[:, :], st_diff[:, :], st_diff[:, :], ALU.mult)
                    pool.tensor_tensor(st_within[:, :], st_sum[:, :, 1], inv_n[:, :],
                                       ALU.mult).then_inc(st_parts_done, 1)
                    pool.wait_ge(constants_made, 1)
                    pool.wait_ge(st_parts_done, g + 1)
                    pool.tensor_scalar(st_between[:, :], st_diff2[:, :], 0.25, EPS, ALU.mult,
                                       ALU.add).then_inc(st_between_done, 1)
                    pool.wait_ge(st_between_done, g + 1)
                    pool.tensor_tensor(st_var[:, :], st_within[:, :], st_between[:, :],
                                       ALU.add).then_inc(st_var_done, 1)
                    need(pool, z_done, g - SLOTS + 1)
                    pool.wait_ge(st_var_done, g + 1)
                    for half, cols in enumerate((slice(0, PAIRS), slice(PAIRS, 3 * PAIRS))):
                        count = 2 * g + 1 + half
                        pool.tensor_tensor(rstd0[:, slot, cols], st_var[:, cols], minus_half[:, cols],
                                           ALU.pow).then_inc(st_rstd_done, 1)
                        pool.wait_ge(st_rstd_done, count)
                        pool.tensor_tensor(st_sr[:, cols], st_sum[:, cols, 0], rstd0[:, slot, cols],
                                           ALU.mult).then_inc(st_sr_done, 1)
                        pool.wait_ge(constants_made, 1)
                        pool.wait_ge(st_sr_done, count)
                        pool.tensor_scalar(shift0[:, slot, cols], st_sr[:, cols], -0.5, 1.0, ALU.mult,
                                           ALU.add).then_inc(shift0_done, 1)

                    def of_cf(st):
                        return (st[:, slot, PAIRS:3 * PAIRS].rearrange("p (h a) -> p a h", h=2)
                                .unsqueeze(3).broadcast_to([P, PAIRS, 2, C]))

                    pool.tensor_tensor(cf_scaled[:, :, :, :], cf_sb[:, slot, :, :, :], of_cf(rstd0),
                                       ALU.mult).then_inc(cf_scaled_done, 1)
                    pool.wait_ge(shift0_done, 2 * g + 2)
                    need(pool, mix0_made, g - SLOTS + 1)
                    pool.wait_ge(cf_scaled_done, g + 1)
                    pool.tensor_tensor(cfn_sb[:, slot, :, :, :], cf_scaled[:, :, :, :], of_cf(shift0),
                                       ALU.add).then_inc(cfn_done, 1)
                g, slot = n - LAG_MIX, (k - LAG_MIX) % SLOTS
                if live(n, LAG_MIX):
                    if isinstance(n, int) and n == LAG_MIX:
                        pool.wait_ge(late_folds_copied, upto_late("row_bias"))
                    need(pool, x1_done, g)
                    pool.wait_ge(res_done, g + 1)
                    pool.tensor_tensor(resb_sb[:, :, :], res_sb[:, slot, :, :],
                                       row_bias[:, :].unsqueeze(1).broadcast_to([P, PAIRS, D]),
                                       ALU.add).then_inc(resb_done, 1)
                    pool.wait_ge(s1_var_done, g + 1)
                    pool.tensor_tensor(rstd1[:, :], s1_var[:, :], minus_half[:, 0:PAIRS],
                                       ALU.pow).then_inc(rstd1_done, 1)

            schedule(pool, step)

        @block.scalar
        def _(act):
            act.wait_ge(constants_made, 1)
            nc.scalar.activation(warm[:, :], ones[0:1, 0:1], ACT.Exp)

            def copy_late_folds(n, first, last):
                if not (isinstance(n, int) and n == LAG_SCORE):
                    return
                for name, dst, src, scale, bias in (
                        ("wvT_a", wvT["a"][:, :], fold_ps("wvT_a")[:, 0:C], 1.0, col(cols128_c, "a_bv")),
                        ("wvT_v", wvT["v"][:, :], fold_ps("wvT_v")[:, 0:C], 1.0, col(cols128_c, "v_bv")),
                        ("out1_bias", out1_bias[:, :], fold_ps("out1_bias")[:, 0:1], 1.0, col(cols128_sb, "1_bo")),
                        ("w_fc", w_fc[:, :], fold_ps("w_fc"), 1.0, None),
                        ("row_bias", row_bias[:, :], fold_ps("row_bias"), 1.0, None),
                        ("m1", m1[:, :], fold_ps("m1")[:, 0:C + 1], SCALE, None),
                        ("w0_a", w0[0:C, :], fold_ps("w0_a")[0:C, :], 1.0, None),
                        ("w0_v", w0[C:2 * C, :], fold_ps("w0_v")[C:2 * C, :], 1.0, None),
                        ("w1", w1[:, :], fold_ps("w1"), 1.0, None),
                        ("bq1", bq1[:, :], fold_ps("bq1")[:, 0:1], -1.0, col(cols128_sb, "1_bq")),
                        ("t1_bias", t1_bias[:, :], fold_ps("t1_bias")[0:C + 1, 0:1], SCALE, None)):
                    if not upto(first) <= upto(name) <= upto(last):
                        continue
                    act.wait_ge(folds_made, upto(name))
                    if bias is None:
                        nc.scalar.mul(dst, src, scale).then_inc(late_folds_copied, 1)
                    else:
                        nc.scalar.activation(dst, src, ACT.Identity, bias=bias, scale=scale
                                             ).then_inc(late_folds_copied, 1)

            def step(n, k):
                draining = isinstance(n, int) and n > LAG_MIX and not live(n, LAG_MIX)

                def mix1():
                    g = n - LAG_ATT1
                    if live(n, LAG_ATT1):
                        act.wait_ge(mix1_made, g + 1)
                        nc.scalar.copy(mix1_sb[:, :, :, :], by_batch(ps_g1[:, 0:DUOS * P], DUOS)
                                       ).then_inc(mix1_copied, 1)

                g = n - LAG_SCORE
                if live(n, LAG_SCORE):
                    act.wait_ge(zT_made, g + 1)
                    nc.scalar.copy(zT_sb[:, :, :, :], by_batch(ps_z[:, :])).then_inc(zT_copied, 1)
                    copy_late_folds(n, "wvT_a", "w_fc")
                    act.wait_ge(cfT_made, g + 1)
                    nc.scalar.copy(cfT_sb[:, :, :, :], by_batch(ps_s0[:, :])).then_inc(cfT_copied, 1)
                g = n - LAG_DENSE
                if live(n, LAG_DENSE):
                    act.wait_ge(resT_made, g + 1)
                    nc.scalar.copy(resT_sb[:, :, :], by_pair(ps_s1[:, :])).then_inc(resT_copied, 1)
                g = n - LAG_SCORE
                if live(n, LAG_SCORE):
                    act.wait_ge(t0_made, g + 1)
                    nc.scalar.copy(t0_sb[:, :, :, :], by_batch(ps_z[:, :])).then_inc(t0_copied, 1)
                    copy_late_folds(n, "row_bias", "m1")
                g = n - LAG_MIX
                if live(n, LAG_MIX):
                    act.wait_ge(prob0T_made, g + 1)
                    nc.scalar.copy(prob0T_sb[:, :, :, :], by_batch(ps_o0[:, :])).then_inc(prob0T_copied, 1)
                g = n - LAG_ATT1
                if live(n, LAG_ATT1):
                    act.wait_ge(max1_done, g + 1)
                    need(act, rsum1_done, g)
                    for p in range(PAIRS):
                        last = nc.scalar.activation(exp1[:, p, :], ps_s1[:, p * S:(p + 1) * S], ACT.Exp,
                                                    bias=minus_max1[:, p:p + 1], accum_out=sum1[:, p:p + 1])
                    last.then_inc(exp1_done, 1)
                g = n - LAG_MIX
                if live(n, LAG_MIX):
                    act.wait_ge(mix0_made, g + 1)
                    nc.scalar.copy(mix0_sb[:, :, :, :].rearrange("p a b s -> p b a s"),
                                   ps_g[:, :, 0:PAIRS * S].rearrange("p b (a s) -> p b a s", a=PAIRS)
                                   ).then_inc(mix0_copied, 1)
                g = n - LAG_ATT1
                if live(n, LAG_ATT1):
                    act.wait_ge(prob1T_made, g + 1)
                    nc.scalar.copy(prob1T_sb[:, :, :, :], by_batch(ps_g1[:, 0:DUOS * P], DUOS)
                                   ).then_inc(prob1T_copied, 1)
                if draining:
                    mix1()
                g = n - LAG_DENSE
                if live(n, LAG_DENSE):
                    act.wait_ge(x1T_made, g + 1)
                    nc.scalar.copy(x1T_sb[:, :, :, :], by_batch(ps_d[:, :])).then_inc(x1T_copied, 1)
                g, slot = n - LAG_NORM, (k - LAG_NORM) % SLOTS
                if live(n, LAG_NORM):
                    act.wait_ge(x_in[slot], landed(g, slot))
                    act.wait_ge(shift0_done, 2 * g + 1)
                    for p in range(PAIRS):
                        last = nc.scalar.activation(z_sb[:, slot, p, :], x_sb[:, slot, p, :], ACT.Identity,
                                                    bias=shift0[:, slot, p:p + 1], scale=rstd0[:, slot, p:p + 1])
                    last.then_inc(z_done, 1)
                copy_late_folds(n, "w0_a", "t1_bias")
                if not draining:
                    mix1()
                g = n - LAG_DENSE
                if live(n, LAG_DENSE):
                    act.wait_ge(t1_made, g + 1)
                    nc.scalar.activation(t1_sb[:, :, :, :], by_batch(ps_d[0:C + 1, :]), ACT.Identity,
                                         bias=t1_bias[:, :]).then_inc(t1_copied, 1)
                g = n - LAG_SCORE
                if live(n, LAG_SCORE):
                    act.wait_ge(diff0_done, g + 1)
                    nc.scalar.activation(exp0[:, :, :], diff0[:, :, :], ACT.Exp).then_inc(exp0_done, 1)

            schedule(act, step)

        @block.vector
        def _(dve):
            v = nc.vector

            def wide(ap, n):
                return ap.unsqueeze(2).broadcast_to([P, n, S])

            def stats_cf(g, slot, h):
                if h == 0:
                    dve.wait_ge(cf_in[slot], landed(g, slot))
                    need(dve, st_sr_done, 2 * (g - SLOTS + 1))
                for p in range(PAIRS):
                    v.bn_stats(stats0[:, slot, (1 + h) * PAIRS + p, :], cf_sb[:, slot, p, h, :])

            def stats_x(g, slot):
                dve.wait_ge(x_in[slot], landed(g, slot))
                for p in range(PAIRS):
                    last = v.bn_stats(stats0[:, slot, p, :], x_sb[:, slot, p, :])
                last.then_inc(stats0_done, 1)

            v.memset(ct_sb[C:C + 1, :, :, :, :], 1.0).then_inc(ct_ones_made, 1)
            stats_cf(0, 0, 0)
            stats_cf(0, 0, 1)
            stats_x(0, 0)
            dve.wait_ge(constants_made, 1)
            v.tensor_scalar_add(centre128[:, :], ident[:, :], -1.0 / D)
            v.tensor_scalar_add(centre64[:, :], ident[0:C, 0:C], -1.0 / C)
            dve.wait_ge(first_weights_in, 16 * FIRST_LOADS)
            v.tensor_scalar_mul(cols128_d[:, :], cols128_sb[:, :], 1.0 / D)
            v.tensor_scalar_mul(cols128_c[:, :], cols128_sb[:, :], 1.0 / C)
            v.tensor_scalar_mul(cols64_c[:, :], cols64_sb[:, :], 1.0 / C).then_inc(scaled_made, 1)
            dve.wait_ge(scaled_made, 1)
            for name, s in (("a1", "a_ln1"), ("v1", "v_ln1")):
                v.tensor_scalar(affine[name][:, :], centre128[:, :], col(cols128_sb, s + "_g"),
                                col(cols128_d, s + "_b"), ALU.mult, ALU.add)
            for name, s in (("a2", "a_ln2"), ("v2", "v_ln2")):
                last = v.tensor_scalar(affine[name][:, :], centre64[:, :], col(cols64_sb, s + "_g", COLS64),
                                       col(cols64_c, s + "_b", COLS64), ALU.mult, ALU.add)
            last.then_inc(affines_made, 1)
            v.tensor_scalar_mul(affine["ln"][:, :], centre128[:, :], col(cols128_sb, "ln_g"))
            v.tensor_scalar_mul(ln_b_wide[:, :], ones[:, :], col(cols128_sb, "ln_b"))
            v.tensor_scalar_mul(bv1_wide[:, :], ones[:, :], col(cols128_sb, "1_bv"))
            v.tensor_copy(wk1T[:, C:C + 1], col(cols128_sb, "1_bk"))
            for s in "av":
                dve.wait_ge(folds_made, upto(f"wqT_{s}"))
                v.tensor_scalar_add(wqT[s][:, :], fold_ps(f"wqT_{s}"), col(cols128_d, f"{s}_bq")
                                    ).then_inc(folds_copied, 1)
                dve.wait_ge(folds_made, upto(f"wkT_{s}"))
                v.tensor_scalar_add(wkT[s][:, :], fold_ps(f"wkT_{s}")[:, 0:C], col(cols128_c, f"{s}_bk")
                                    ).then_inc(folds_copied, 1)
            for s, at in (("a", 0), ("v", C)):
                dve.wait_ge(folds_made, upto(f"m0_{s}"))
                v.tensor_scalar_mul(m0[:, at:at + C], fold_ps(f"m0_{s}")[:, 0:C], SCALE).then_inc(folds_copied, 1)
            dve.wait_ge(late_weights_in, 16 * LATE_LOADS)
            v.tensor_copy(wk1T[:, 0:C], wt_sb[:, 0, :]).then_inc(affines_made, 1)

            def step(n, k):

                g = n - LAG_MIX
                if live(n, LAG_MIX):
                    dve.wait_ge(exp0_done, g + 1)
                    v.tensor_reduce(sum0[:, :], exp0[:, :, :], AX.X, ALU.add).then_inc(sum0_done, 1)
                    dve.wait_ge(sum0_done, g + 1)
                    v.reciprocal(rsum0[:, :], sum0[:, :]).then_inc(rsum0_done, 1)
                if live(n, LAG_MIX):
                    dve.wait_ge(rsum0_done, g + 1)
                    v.tensor_tensor(prob0[:, :, :], exp0[:, :, :], wide(rsum0[:, :], 2 * PAIRS),
                                    ALU.mult).then_inc(prob0_done, 1)
                g, slot = n - LAG_FINAL, (k - LAG_FINAL) % SLOTS
                if live(n, LAG_FINAL):
                    dve.wait_ge(out1_made, g + 1)
                    dve.wait_ge(rsum1_done, g + 1)
                    if not (isinstance(g, int) and g < SLOTS):
                        dve.wait_ge(out_stored[slot], landed(g - SLOTS, slot))
                    for p in range(PAIRS):
                        last = v.scalar_tensor_tensor(
                            out_sb[:, slot, p, :], ps_g[:, p % 2, (p // 2) * D:(p // 2 + 1) * D],
                            rsum1[:, p:p + 1], x1_sb[:, slot, p, :], ALU.mult, ALU.add)
                    last.then_inc(final_done, 1)
                g = n - LAG_ATT1
                if live(n, LAG_ATT1):
                    dve.wait_ge(s1_made, g + 1)
                    v.tensor_reduce(minus_max1[:, :], by_pair(ps_s1[:, 0:PAIRS * S]), AX.X, ALU.max,
                                    negate=True).then_inc(max1_done, 1)
                if live(n, LAG_STATS):
                    stats_cf(n, k, 0)
                g, slot = n - LAG_DENSE, (k - LAG_DENSE) % SLOTS
                if live(n, LAG_DENSE):
                    dve.wait_ge(dense_made, g + 1)
                    dve.wait_ge(rstd1_done, g + 1)
                    dve.wait_ge(resb_done, g + 1)
                    need(dve, final_done, g - SLOTS + 1)
                    for p in range(PAIRS):
                        last = v.scalar_tensor_tensor(x1_sb[:, slot, p, :], ps_d[:, p * D:(p + 1) * D],
                                                      rstd1[:, p:p + 1], resb_sb[:, p, :], ALU.mult, ALU.add)
                    last.then_inc(x1_done, 1)
                if live(n, LAG_STATS):
                    stats_cf(n, k, 1)
                g = n - LAG_ATT1
                if live(n, LAG_ATT1):
                    need(dve, final_done, g)
                    dve.wait_ge(exp1_done, g + 1)
                    v.reciprocal(rsum1[:, :], sum1[:, :]).then_inc(rsum1_done, 1)
                if live(n, LAG_STATS):
                    stats_x(n, k)
                g = n - LAG_SCORE
                if live(n, LAG_SCORE):
                    dve.wait_ge(s0_made, g + 1)
                    v.tensor_reduce(max0[:, :], ps_s0[:, :].rearrange("p (a s) -> p a s", a=2 * PAIRS), AX.X,
                                    ALU.max).then_inc(max0_done, 1)
                    dve.wait_ge(max0_done, g + 1)
                    v.tensor_tensor(diff0[:, :, :], ps_s0[:, :].rearrange("p (a s) -> p a s", a=2 * PAIRS),
                                    wide(max0[:, :], 2 * PAIRS), ALU.subtract).then_inc(diff0_done, 1)
                g, slot = n - LAG_MIX, (k - LAG_MIX) % SLOTS
                if live(n, LAG_MIX):
                    dve.wait_ge(out0_made, g + 1)
                    dve.wait_ge(xres_in[slot], landed(g, slot))
                    v.tensor_tensor(res_sb[:, slot, :, :], by_pair(ps_o0[:, :]), xres_sb[:, slot, :, :],
                                    ALU.add).then_inc(res_done, 1)
                    dve.wait_ge(res_done, g + 1)
                    for p in range(PAIRS):
                        last = v.bn_stats(stats1[:, p, :], res_sb[:, slot, p, :])
                    last.then_inc(stats1_done, 1)
                    dve.wait_ge(stats1_done, g + 1)
                    v.tensor_tensor(s1_m2[:, :], stats1[:, :, 2], stats1[:, :, 5], ALU.add)
                    v.tensor_tensor(s1_diff[:, :], stats1[:, :, 1], stats1[:, :, 4],
                                    ALU.subtract).then_inc(s1_sums_done, 1)
                    dve.wait_ge(s1_sums_done, g + 1)
                    v.tensor_tensor(s1_diff2[:, :], s1_diff[:, :], s1_diff[:, :], ALU.mult)
                    v.tensor_scalar(s1_within[:, :], s1_m2[:, :], 1.0 / D, EPS, ALU.mult,
                                    ALU.add).then_inc(s1_parts_done, 1)
                    dve.wait_ge(s1_parts_done, g + 1)
                    v.scalar_tensor_tensor(s1_var[:, :], s1_diff2[:, :], 0.25, s1_within[:, :], ALU.mult,
                                           ALU.add).then_inc(s1_var_done, 1)

            schedule(dve, step)

        @block.tensor
        def _(pe):
            mm = nc.tensor.matmul
            pe.wait_ge(constants_made, 1)
            pe.wait_ge(first_weights_in, 16 * FIRST_LOADS)
            pe.wait_ge(affines_made, 1)
            for s in "av":
                mm(fold_ps(f"wqT_{s}"), w(f"{s}_Wq"), affine[f"{s}1"][:, :], start=True, stop=True
                   ).then_inc(folds_made, 1)
                mm(fold_ps(f"wkT_{s}")[:, 0:C], wc(f"{s}_Wk"), affine[f"{s}2"][:, :], start=True, stop=True
                   ).then_inc(folds_made, 1)
            for s in "av":
                pe.wait_ge(folds_copied, upto(f"wkT_{s}"))
                mm(fold_ps(f"m0_{s}")[:, 0:C], wqT[s][:, :], wkT[s][:, :], start=True, stop=True
                   ).then_inc(folds_made, 1)

            def late_folds_1(n):
                if not (isinstance(n, int) and n == LAG_SCORE):
                    return
                pe.wait_ge(affines_made, 2)
                pe.wait_ge(late_weights_in, 16 * LATE_LOADS)
                for s in "av":
                    mm(fold_ps(f"wvT_{s}")[:, 0:C], wc(f"{s}_Wv"), affine[f"{s}2"][:, :], start=True, stop=True
                       ).then_inc(folds_made, 1)
                mm(fold_ps("out1_bias")[:, 0:1], w("1_Wo"), col(cols128_sb, "1_bv"), start=True, stop=True
                   ).then_inc(folds_made, 1)
                mm(fold_ps("w_fc"), affine["ln"][:, :], w("fc_W"), start=True, stop=True).then_inc(folds_made, 1)

            def late_folds_2(n):
                if not (isinstance(n, int) and n == LAG_SCORE):
                    return
                dst = fold_ps("row_bias")
                mm(dst, ln_b_wide[:, :], w("fc_W"), start=True, stop=False)
                mm(dst, bv1_wide[:, :], w("1_Wo"), start=False, stop=False)
                mm(dst, ones[0:1, :], row("fc_b"), start=False, stop=False)
                mm(dst, ones[0:1, :], row("1_bo"), start=False, stop=True).then_inc(folds_made, 1)
                mm(fold_ps("m1")[:, 0:C + 1], w("1_WqT"), wk1T[:, :], start=True, stop=True
                   ).then_inc(folds_made, 1)

            def late_folds_3(n):
                if not (isinstance(n, int) and n == LAG_SCORE):
                    return
                for s, at in (("a", 0), ("v", C)):
                    pe.wait_ge(late_folds_copied, upto_late(f"wvT_{s}"))
                    dst = fold_ps(f"w0_{s}")[at:at + C, :]
                    mm(dst, wvT[s][:, :], w(f"{s}_Wo"), start=True, stop=False)
                    mm(dst, part64[:, :], row(f"{s}_bo"), start=False, stop=True).then_inc(folds_made, 1)
                pe.wait_ge(late_folds_copied, upto_late("out1_bias"))
                mm(fold_ps("w1"), wt_sb[:, 1:3, :], w("1_Wo"), start=True, stop=True).then_inc(folds_made, 1)
                pe.wait_ge(late_folds_copied, upto_late("w_fc"))
                mm(fold_ps("bq1")[:, 0:1], w("1_Wq"), out1_bias[:, :], start=True, stop=True
                   ).then_inc(folds_made, 1)
                pe.wait_ge(late_folds_copied, upto_late("bq1"))
                mm(fold_ps("t1_bias")[0:C + 1, 0:1], wk1T[:, :], bq1[:, :], start=True, stop=True
                   ).then_inc(folds_made, 1)

            LOW, HIGH = slice(0, C), slice(C, 2 * C)

            def step(n, k):
                score_g, score_slot = n - LAG_SCORE, (k - LAG_SCORE) % SLOTS
                mix_g, mix_slot = n - LAG_MIX, (k - LAG_MIX) % SLOTS
                dense_g, dense_slot = n - LAG_DENSE, (k - LAG_DENSE) % SLOTS
                att1_g, att1_slot = n - LAG_ATT1, (k - LAG_ATT1) % SLOTS
                draining = isinstance(n, int) and n > LAG_MIX and not live(n, LAG_MIX)

                def mix1():
                    if live(n, LAG_ATT1):
                        pe.wait_ge(folds_made, 1)
                        pe.wait_ge(prob1T_copied, att1_g + 1)
                        pe.wait_ge(c1_in[att1_slot], landed(att1_g, att1_slot))
                        for q in range(DUOS):
                            for b in range(2):
                                for half in (LOW, HIGH):
                                    last = mm(ps_g1[half, (2 * q + b) * S:(2 * q + b + 1) * S],
                                              c1_sb[half, att1_slot, q, b, :], prob1T_sb[half, q, b, :],
                                              start=True, stop=True)
                        last.then_inc(mix1_made, 1)

                def x1T():
                    if live(n, LAG_DENSE):
                        pe.wait_ge(x1_done, dense_g + 1)
                        for p in range(PAIRS):
                            last = nc.tensor.transpose(ps_d[:, p * P:(p + 1) * P], x1_sb[:, dense_slot, p, :],
                                                       ident[:, :])
                        last.then_inc(x1T_made, 1)

                def out1():
                    if live(n, LAG_ATT1):
                        if not live(n, LAG_MIX):
                            need(pe, final_done, att1_g)
                        pe.wait_ge(mix1_copied, att1_g + 1)
                        for q in range(DUOS):
                            for h, half in ((0, LOW), (1, HIGH)):
                                last = mm(ps_g[:, h, q * D:(q + 1) * D], mix1_sb[half, q, :, :], w1[half, :],
                                          start=True, stop=True)
                        last.then_inc(out1_made, 1)

                def t1():
                    if live(n, LAG_DENSE):
                        pe.wait_ge(x1T_copied, dense_g + 1)
                        mm(ps_d[0:C + 1, :], m1[:, :], x1T_sb[:, :, :, :], start=True, stop=True
                           ).then_inc(t1_made, 1)

                if live(n, LAG_SCORE):
                    pe.wait_ge(z_done, score_g + 1)
                    for p in range(PAIRS):
                        last = nc.tensor.transpose(ps_z[:, p * P:(p + 1) * P], z_sb[:, score_slot, p, :],
                                                   ident[:, :])
                    last.then_inc(zT_made, 1)
                    late_folds_1(n)
                    pe.wait_ge(cfn_done, score_g + 1)
                    need(pe, diff0_done, score_g)
                    for p in range(PAIRS):
                        last = nc.tensor.transpose(ps_s0[:, p * P:(p + 1) * P], cfn_sb[:, score_slot, p, :, :],
                                                   ident[:, :])
                    last.then_inc(cfT_made, 1)
                if live(n, LAG_DENSE):
                    pe.wait_ge(res_done, dense_g + 1)
                    for p in range(PAIRS):
                        last = nc.tensor.transpose(ps_s1[:, p * P:(p + 1) * P], res_sb[:, dense_slot, p, :],
                                                   ident[:, :])
                    last.then_inc(resT_made, 1)
                if live(n, LAG_SCORE):
                    pe.wait_ge(zT_copied, score_g + 1)
                    if isinstance(n, int) and n == LAG_SCORE:
                        pe.wait_ge(folds_copied, N_SCORE_FOLDS)
                    mm(ps_z[:, :], m0[:, :], zT_sb[:, :, :, :], start=True, stop=True).then_inc(t0_made, 1)
                    late_folds_2(n)
                if live(n, LAG_ATT1):
                    if isinstance(n, int) and n == LAG_ATT1:
                        pe.wait_ge(ct_ones_made, 1)
                    pe.wait_ge(t1_copied, att1_g + 1)
                    pe.wait_ge(ct_in[att1_slot], landed(att1_g, att1_slot))
                    need(pe, resT_copied, dense_g + 1)
                    for p in range(PAIRS):
                        for b in range(2):
                            last = mm(ps_s1[b * S:(b + 1) * S, p * S:(p + 1) * S], t1_sb[:, p, b, :],
                                      ct_sb[:, att1_slot, p, b, :], start=True, stop=True)
                    last.then_inc(s1_made, 1)
                if live(n, LAG_MIX):
                    if isinstance(n, int) and n == LAG_MIX:
                        pe.wait_ge(late_folds_copied, N_LATE_FOLDS)
                    pe.wait_ge(prob0_done, mix_g + 1)
                    for p in range(PAIRS):
                        last = nc.tensor.transpose(ps_o0[:, p * P:(p + 1) * P], prob0[:, 2 * p:2 * p + 2, :],
                                                   ident[:, :])
                    last.then_inc(prob0T_made, 1)
                if live(n, LAG_DENSE):
                    pe.wait_ge(resT_copied, dense_g + 1)
                    for p in range(PAIRS):
                        last = mm(ps_d[:, p * P:(p + 1) * P], resT_sb[:, p, :], w_fc[:, :], start=True, stop=True)
                    last.then_inc(dense_made, 1)
                if live(n, LAG_MIX):
                    pe.wait_ge(folds_made, 1)
                    need(pe, final_done, n - LAG_FINAL + 1)
                    pe.wait_ge(prob0T_copied, mix_g + 1)
                    for p in range(PAIRS):
                        for h, b in ((0, 0), (1, 1), (1, 0), (0, 1)):
                            last = mm(ps_g[h * C:(h + 1) * C, b, p * S:(p + 1) * S],
                                      cfn_sb[b * S:(b + 1) * S, mix_slot, p, h, :],
                                      prob0T_sb[b * S:(b + 1) * S, p, h, :], start=True, stop=True)
                    last.then_inc(mix0_made, 1)
                if live(n, LAG_ATT1):
                    pe.wait_ge(exp1_done, att1_g + 1)
                    for q in range(DUOS):
                        last = nc.tensor.transpose(ps_g1[:, q * P:(q + 1) * P], exp1[:, 2 * q:2 * q + 2, :],
                                                   ident[:, :])
                    last.then_inc(prob1T_made, 1)
                if draining:
                    mix1()
                x1T()
                if live(n, LAG_SCORE):
                    pe.wait_ge(folds_made, 1)
                    pe.wait_ge(cfT_copied, score_g + 1)
                    pe.wait_ge(t0_copied, score_g + 1)
                    for p in range(PAIRS):
                        for b in range(2):
                            for half in (LOW, HIGH):
                                last = mm(ps_s0[half, (2 * p + b) * S:(2 * p + b + 1) * S],
                                          t0_sb[half, p, b, :], cfT_sb[half, p, b, :], start=True, stop=True)
                    last.then_inc(s0_made, 1)
                    late_folds_3(n)
                if live(n, LAG_MIX):
                    pe.wait_ge(mix0_copied, mix_g + 1)
                    for p in range(PAIRS):
                        last = mm(ps_o0[:, p * P:(p + 1) * P], mix0_sb[:, p, :, :], w0[:, :], start=True, stop=True)
                    last.then_inc(out0_made, 1)
                if draining:
                    out1()
                    t1()
                else:
                    mix1()
                    t1()
                    out1()

            schedule(pe, step)


def kernel(**inputs):
    from concourse import bacc
    from concourse.bass_utils import run_bass_kernel_spmd

    a = {k: np.asarray(v) for k, v in inputs.items()}

    def take(name):
        return a["L1_xattn_" + name[2:]] if name.startswith("1_") else a["L0_xattn_" + name]

    def by_pairs(t):
        t = t.reshape(GROUPS, PAIRS, 2 * S, t.shape[-1])
        return np.ascontiguousarray(t.transpose(0, 2, 1, 3))

    x, c, f = a["x"], a["ctx_512"], a["fside_BxSxS_0"]
    c_groups = c.reshape(GROUPS, PAIRS, 2, S, C)
    arrays = {
        "x": by_pairs(x),
        "cf": by_pairs(np.concatenate([c, f], axis=-1)).reshape(GROUPS, P, PAIRS, 2, C),
        "ct": np.ascontiguousarray(c_groups.transpose(0, 4, 1, 2, 3)),
        "c1": np.ascontiguousarray(c.reshape(GROUPS, DUOS, 2, 2, S, C).transpose(0, 2, 4, 1, 3, 5)
                                   .reshape(GROUPS, P, DUOS, 2, C)),
        "w_score": np.ascontiguousarray(np.stack([take(n) for n in W_SCORE], axis=1)),
        "w64": np.ascontiguousarray(np.stack([take(n) for n in W64], axis=1)),
        "w128": np.ascontiguousarray(np.stack(
            [take(n[:-1]).T if n.endswith("T") else take(n) for n in W128], axis=1)),
        "wt": np.ascontiguousarray(np.stack([take(n[:-1]).T for n in WT], axis=1)),
        "cols128": np.ascontiguousarray(np.stack([take(n) for n in COLS128], axis=1)),
        "cols64": np.ascontiguousarray(np.stack([take(n) for n in COLS64], axis=1)),
        "rows": np.ascontiguousarray(np.stack([take(n) for n in ROWS])[None]),
    }
    nc = bacc.Bacc("TRN2", target_bir_lowering=False, num_devices=1)
    args = [nc.dram_tensor(f"in_{n}", v.shape, mybir.dt.from_np(v.dtype), kind="ExternalInput").ap()
            for n, v in arrays.items()]
    out = nc.dram_tensor("out", (GROUPS, P, PAIRS, D), F32, kind="ExternalOutput").ap()
    attention_kernel(nc, *args, out)
    r = run_bass_kernel_spmd(nc, [{f"in_{n}": v for n, v in arrays.items()}], core_ids=[0])
    got = np.asarray(r.results[0]["out"]).reshape(GROUPS, P, PAIRS, D)
    return np.ascontiguousarray(got.transpose(0, 2, 1, 3)).reshape(BATCH, S, D)
```
